# Optimizing a Trainium2 kernel written in Bass

```python
import numpy as np
import jax
import jax.numpy as jnp

def _softmax(x, axis=-1):
    return jax.nn.softmax(x, axis=axis)

def _gelu(x):
    return jax.nn.gelu(x, approximate=True)

def _silu(x):
    return jax.nn.silu(x)

def _sigmoid(x):
    return jax.nn.sigmoid(x)

def _layernorm(x, axis=-1, eps=1e-05):
    m = jnp.mean(x, axis=axis, keepdims=True)
    v = jnp.var(x, axis=axis, keepdims=True)
    return (x - m) / jnp.sqrt(v + eps)

def _scatter_add(tgt, idx, src, axis=0):
    return tgt.at[idx].add(src)

def _segment_sum(src, seg, n):
    return jax.ops.segment_sum(src, seg, n)
kernel_name = 'mk_seq_preln_d1_jaxref_r8_8eff33'

def setup_inputs(seed: int=0):
    np.random.seed(seed)
    _w = jnp.asarray

    def _L0_attn_setup():
        import jax, jax.numpy as jnp
        import numpy as np
        B, L, E, H = (2, 256, 128, 16)
        HD = E // H
        THETA = 10000.0

        def _rope_tables(seq_len, dim, dtype):
            inv_freq = 1.0 / THETA ** (jnp.arange(0, dim, 2, dtype=jnp.float32) / dim)
            freqs = jnp.arange(seq_len, dtype=jnp.float32)[:, None] * inv_freq[None, :]
            freqs = jnp.repeat(freqs, 2, axis=-1)
            return (jnp.cos(freqs).astype(dtype), jnp.sin(freqs).astype(dtype))

        def _rotate_half(x):
            x2 = x.reshape(*x.shape[:-1], -1, 2)
            x2 = jnp.stack([-x2[..., 1], x2[..., 0]], axis=-1)
            return x2.reshape(x.shape)

        def _apply_rope(x, cos, sin):
            return x * cos[None, None] + _rotate_half(x) * sin[None, None]
        key = jax.random.key(seed)
        ks = jax.random.split(key, 9)
        s = 1.0 / np.sqrt(E)
        return {'x': jax.random.normal(ks[0], (B, L, E), jnp.float32), 'Wq': jax.random.normal(ks[1], (E, E), jnp.float32) * s, 'bq': jax.random.normal(ks[2], (E,), jnp.float32) * 0.01, 'Wk': jax.random.normal(ks[3], (E, E), jnp.float32) * s, 'bk': jax.random.normal(ks[4], (E,), jnp.float32) * 0.01, 'Wv': jax.random.normal(ks[5], (E, E), jnp.float32) * s, 'bv': jax.random.normal(ks[6], (E,), jnp.float32) * 0.01, 'Wo': jax.random.normal(ks[7], (E, E), jnp.float32) * s, 'bo': jax.random.normal(ks[8], (E,), jnp.float32) * 0.01}
    _L0_attn_in = _L0_attn_setup()

    def _L0_ffn_setup():
        import jax, jax.numpy as jnp
        import numpy as np
        B, S, D, H, E, K = (4, 256, 128, 512, 8, 2)
        CAPACITY_FACTOR = 1.5
        C = int(CAPACITY_FACTOR * B * S * K / E)
        key = jax.random.key(seed)
        ks = jax.random.split(key, 6)
        x = jax.random.normal(ks[0], (B, S, D), dtype=jnp.float32)
        w_router = jax.random.normal(ks[1], (D, E), dtype=jnp.float32) * 0.02
        w1 = jax.random.normal(ks[2], (E, D, H), dtype=jnp.float32) * 0.02
        b1 = jnp.zeros((E, H), dtype=jnp.float32)
        w2 = jax.random.normal(ks[3], (E, H, D), dtype=jnp.float32) * 0.02
        b2 = jnp.zeros((E, D), dtype=jnp.float32)
        return {'x': x, 'w_router': w_router, 'w1': w1, 'b1': b1, 'w2': w2, 'b2': b2}
    _L0_ffn_in = _L0_ffn_setup()
    _d = {'L0_attn_x': _L0_attn_in['x'], 'L0_attn_Wq': _L0_attn_in['Wq'], 'L0_attn_bq': _L0_attn_in['bq'], 'L0_attn_Wk': _L0_attn_in['Wk'], 'L0_attn_bk': _L0_attn_in['bk'], 'L0_attn_Wv': _L0_attn_in['Wv'], 'L0_attn_bv': _L0_attn_in['bv'], 'L0_attn_Wo': _L0_attn_in['Wo'], 'L0_attn_bo': _L0_attn_in['bo'], 'L0_ffn_w_router': _L0_ffn_in['w_router'], 'L0_ffn_w1': _L0_ffn_in['w1'], 'L0_ffn_b1': _L0_ffn_in['b1'], 'L0_ffn_w2': _L0_ffn_in['w2'], 'L0_ffn_b2': _L0_ffn_in['b2']}
    _x0 = _d['L0_attn_x']
    _d['L0_attn_x'] = jax.random.normal(jax.random.fold_in(jax.random.key(seed), 1), (8, 256, 128), dtype=_x0.dtype)
    del _x0
    return _d

def reference(L0_attn_x, L0_attn_Wq, L0_attn_bq, L0_attn_Wk, L0_attn_bk, L0_attn_Wv, L0_attn_bv, L0_attn_Wo, L0_attn_bo, L0_ffn_w_router, L0_ffn_w1, L0_ffn_b1, L0_ffn_w2, L0_ffn_b2):

    def _L0_attn_ref(x, Wq, bq, Wk, bk, Wv, bv, Wo, bo):
        import jax, jax.numpy as jnp
        import numpy as np
        B, L, E, H = (2, 256, 128, 16)
        HD = E // H
        THETA = 10000.0

        def _rope_tables(seq_len, dim, dtype):
            inv_freq = 1.0 / THETA ** (jnp.arange(0, dim, 2, dtype=jnp.float32) / dim)
            freqs = jnp.arange(seq_len, dtype=jnp.float32)[:, None] * inv_freq[None, :]
            freqs = jnp.repeat(freqs, 2, axis=-1)
            return (jnp.cos(freqs).astype(dtype), jnp.sin(freqs).astype(dtype))

        def _rotate_half(x):
            x2 = x.reshape(*x.shape[:-1], -1, 2)
            x2 = jnp.stack([-x2[..., 1], x2[..., 0]], axis=-1)
            return x2.reshape(x.shape)

        def _apply_rope(x, cos, sin):
            return x * cos[None, None] + _rotate_half(x) * sin[None, None]
        b, l, e = x.shape
        q = (x @ Wq.T + bq).reshape(b, l, H, HD).transpose(0, 2, 1, 3)
        k = (x @ Wk.T + bk).reshape(b, l, H, HD).transpose(0, 2, 1, 3)
        v = (x @ Wv.T + bv).reshape(b, l, H, HD).transpose(0, 2, 1, 3)
        cos, sin = _rope_tables(l, HD, x.dtype)
        q = _apply_rope(q, cos, sin)
        k = _apply_rope(k, cos, sin)
        scale = 1.0 / np.sqrt(HD)
        scores = jnp.einsum('bhsd,bhed->bhse', q, k) * scale
        attn = jax.nn.softmax(scores, axis=-1)
        out = jnp.einsum('bhse,bhed->bhsd', attn, v)
        out = out.transpose(0, 2, 1, 3).reshape(b, l, e)
        return out @ Wo.T + bo

    def _L0_ffn_ref(x, w_router, w1, b1, w2, b2):
        import jax, jax.numpy as jnp
        import numpy as np
        B, S, D, H, E, K = (4, 256, 128, 512, 8, 2)
        CAPACITY_FACTOR = 1.5
        C = int(CAPACITY_FACTOR * B * S * K / E)
        Bs, Ss, Ds = x.shape
        N = Bs * Ss
        xf = x.reshape(N, Ds)
        logits = xf @ w_router
        probs = jax.nn.softmax(logits, axis=-1)
        gate, eidx = jax.lax.top_k(probs, K)
        gate = gate / jnp.sum(gate, axis=-1, keepdims=True)
        oh = jax.nn.one_hot(eidx, E, dtype=jnp.float32)
        ohf = oh.reshape(N * K, E)
        pos = jnp.cumsum(ohf, axis=0) - 1.0
        posk = jnp.sum(pos * ohf, axis=-1).reshape(N, K).astype(jnp.int32)
        keep = posk < C
        gate = gate * keep.astype(gate.dtype)
        e_flat = eidx.reshape(-1)
        p_flat = jnp.where(keep, posk, 0).reshape(-1)
        contrib = (xf[:, None, :] * keep[..., None].astype(xf.dtype)).reshape(N * K, Ds)
        expert_in = jnp.zeros((E, C, Ds), dtype=xf.dtype).at[e_flat, p_flat].add(contrib)
        h = jax.nn.relu(jnp.einsum('ecd,edh->ech', expert_in, w1) + b1[:, None, :])
        expert_out = jnp.einsum('ech,eho->eco', h, w2) + b2[:, None, :]
        tok = expert_out[e_flat, p_flat].reshape(N, K, -1)
        y = jnp.sum(tok * gate[..., None], axis=1)
        return y.reshape(Bs, Ss, -1)
    x = L0_attn_x
    x = x + _L0_attn_ref(_layernorm(x, axis=-1), L0_attn_Wq, L0_attn_bq, L0_attn_Wk, L0_attn_bk, L0_attn_Wv, L0_attn_bv, L0_attn_Wo, L0_attn_bo)
    x = x + _L0_ffn_ref(_layernorm(x, axis=-1), L0_ffn_w_router, L0_ffn_w1, L0_ffn_b1, L0_ffn_w2, L0_ffn_b2)
    return x

_drawn_inputs = setup_inputs


def setup_inputs(seed=0):
    import zlib

    import numpy as np

    out = dict(_drawn_inputs(seed))
    spreads = {'L0_ffn_b1': (0.0, 0.436), 'L0_ffn_b2': (0.0, 0.1)}
    factors = {'L0_attn_bq': 30.636, 'L0_attn_bk': 40.832, 'L0_attn_bv': 3.863, 'L0_attn_bo': 4.313}
    for name, (base, spread) in spreads.items():
        noise = np.random.default_rng([zlib.crc32(name.encode()), seed]).standard_normal(out[name].shape)
        drawn = base * np.exp(spread * noise) if base else spread * noise
        out[name] = jnp.asarray(drawn.astype(out[name].dtype))
    for name, factor in factors.items():
        out[name] = (out[name] * factor).astype(out[name].dtype)
    return out
```

```python
import concourse.bass as bass
from concourse import mybir
from contextlib import ExitStack

BATCHES, T, D = 8, 256, 128
HEADS, HD = 16, 8
TILES = T // 128
TOKENS = BATCHES * T
EXPERTS, HIDDEN, TOPK = 8, 512, 2
CAPACITY = int(1.5 * 4 * 256 * TOPK / EXPERTS)
SLOT_TILES = CAPACITY // 128
CHUNKS = HIDDEN // 128
SLOTS = EXPERTS * CAPACITY
ROW = D + 2
NOWHERE = 1 << 20
EPS = 1e-5
HALF = HEADS // 2

PART_ROWS = 3 * HD
SCORE_ROWS = PART_ROWS + 2

W_Q, W_K, W_QS, W_KS, W_V, W_O, W_R = 0, 128, 256, 384, 512, 640, 768
W_BIAS = W_R + EXPERTS
W_BV = W_BIAS + 4
W_COLS = W_BV + 1
C_ID, C_COS, C_SIN, C_UP, C_IOTA = 0, 128, 128 + T, 128 + 2 * T, 256 + 2 * T
C_TOK = C_IOTA + TILES * TOPK * EXPERTS
C_COLS = C_TOK + TILES

V_STEP = 265
V_BASE = [V_STEP * i - 9 * (i % 2) for i in range(4)]
V_COLS = 4 * V_STEP

FIRST, LAST = 1, 4
DVE_LINKS, POOL_LINKS = 28, 26


class Count:

    def __init__(self, per_round):
        self.value, self.offset, self.per_round = 0, 0, per_round

    def in_loop(self):
        return not isinstance(self.offset, int)

    def next(self):
        self.value += 1
        return self.value + self.offset


def build(nc, x, wts, cst, bo, w1, b1, w2, b2, out, rows):
    fp32, fp32r, bf16 = mybir.dt.float32, mybir.dt.float32r, mybir.dt.bfloat16
    i32, u32 = mybir.dt.int32, mybir.dt.uint32
    ALU, ACT, AX = mybir.AluOpType, mybir.ActivationFunctionType, mybir.AxisListType
    ctx = ExitStack()
    with ctx:
        def sb(name, shape, dt=fp32):
            return ctx.enter_context(nc.sbuf_tensor(name, shape, dt))

        def sem(name):
            return ctx.enter_context(nc.semaphore(name))

        bank = [ctx.enter_context(nc.psum_tensor(f"bank{i}", [128, 512], fp32)) for i in range(8)]
        score_ps, max_ps, pv_ps = bank[0:2], bank[2:4], bank[4]
        psA, psB, psC = bank[5], bank[6], bank[7]

        W = sb("W", [128, W_COLS])
        C = sb("C", [128, C_COLS])
        bo_all = sb("bo_all", [128, D])
        ones = sb("ones", [2 * HEADS, T])
        bv_rep = sb("bv_rep", [128, 128])
        attn_bias = sb("attn_bias", [128, D])
        before = sb("before", [128, 128], bf16)
        every = sb("every", [128, 128], bf16)
        minus_half = sb("minus_half", [128, TILES])
        blank = sb("blank", [128, SLOTS // 128, ROW])
        ident = C[:, C_ID:C_ID + 128]

        xin = sb("xin", [128, 2, TILES, D])
        stats1 = sb("stats1", [128, 2, TILES, 6])
        mv1 = sb("mv1", [128, 2, TILES, 2])
        rstd1 = sb("rstd1", [128, 2, TILES])
        shift1 = sb("shift1", [128, 2, TILES])
        xn1 = sb("xn1", [128, 2, TILES, D])
        xT = sb("xT", [128, 2, T])
        rot1 = sb("rot1", [128, 2, T])
        rot2 = sb("rot2", [128, 2, T])
        rope = sb("rope", [128, 2, T])
        parts = sb("parts", [128, 2, 4, T], fp32r)
        QK = [sb(f"QK{p}", [SCORE_ROWS, HEADS, 2, T], fp32r) for p in range(2)]
        VA = sb("VA", [128, 2, V_COLS])
        negmax = sb("negmax", [128, 2, TILES, HALF])
        mparts = sb("mparts", [128, 2, TILES, 2, HALF], fp32r)
        mT = sb("mT", [2 * HALF, 2, T], fp32r)
        P = sb("P", [128, 8, 2 * T])
        O = sb("O", [128, 2, T])
        rsum = sb("rsum", [128, TILES * 8, 2])
        On = sb("On", [128, TILES, D])
        OT = sb("OT", [128, T])
        xres = sb("xres", [128, TILES, D])
        xbias = sb("xbias", [128, TILES, D])
        x1 = sb("x1", [128, TILES, D])
        stats2 = sb("stats2", [128, TILES, 6])
        mv2 = sb("mv2", [128, TILES, 2])
        rstd2 = sb("rstd2", [128, TILES])
        shift2 = sb("shift2", [128, TILES])
        pay = sb("pay", [128, 2, TOPK, TILES, ROW])
        xn2T = sb("xn2T", [128, T])
        best = sb("best", [128, TILES, 8])
        besti = sb("besti", [128, TILES, 8], u32)
        choice = sb("choice", [128, TILES, TOPK])
        gap = sb("gap", [128, TILES])
        e2 = sb("e2", [128, TILES])
        den = sb("den", [128, TILES])
        onehot = sb("onehot", [128, TILES, TOPK, EXPERTS])
        chosen = sb("chosen", [128, TILES, EXPERTS], bf16)
        seen = sb("seen", [128, TILES + 1, EXPERTS], bf16)
        hit = sb("hit", [128, TILES, TOPK, EXPERTS])
        slot = sb("slot", [128, TILES, TOPK])
        over = sb("over", [128, TILES, TOPK])
        base = sb("base", [128, TILES, TOPK])
        dest = sb("dest", [128, 2, TILES, TOPK], i32)
        tok = sb("tok", [128, TILES])

        w1s = sb("w1s", [128, 2, HIDDEN])
        w2s = sb("w2s", [128, 2, CHUNKS, D])
        xe = sb("xe", [128, 4, SLOT_TILES, ROW])
        b1s = sb("b1s", [128, 2, CHUNKS])
        b2s = sb("b2s", [128, 2, D])
        xeT = sb("xeT", [128, 2, CAPACITY])
        hT = sb("hT", [128, CHUNKS, CAPACITY])
        yb = sb("yb", [128, SLOT_TILES, D])
        yg = sb("yg", [128, 2, SLOT_TILES, D])

        wts_in, cst_in, bo_in = sem("wts_in"), sem("cst_in"), sem("bo_in")
        bias_ps, attn_bias_ok, bv_ok, before_ok, va_set, ones_set, ones_in = (
            sem(n) for n in ("bias_ps", "attn_bias_ok", "bv_ok", "before_ok", "va_set", "ones_set", "ones_in"))
        blank_set = sem("blank_set")
        x_in = [sem("x_in0"), sem("x_in1")]
        stats1_ok, xn1_ok = sem("stats1_ok"), sem("xn1_ok")
        xT_ps, xT_ok, qk_ps, qs_ps, qk_ev, qs_ev = (sem(n) for n in ("xT_ps", "xT_ok", "qk_ps", "qs_ps", "qk_ev", "qs_ev"))
        v_ps, v_ok, rope_ok, hi_ok, parts_ok = (sem(n) for n in ("v_ps", "v_ok", "rope_ok", "hi_ok", "parts_ok"))
        moved = [sem("moved0"), sem("moved1")]
        max_ps_ok, max_ok, mparts_ok, mT_ps, mT_ok = (sem(n) for n in ("max_ps_ok", "max_ok", "mparts_ok", "mT_ps", "mT_ok"))
        max_in = [sem("max_in0"), sem("max_in1")]
        score_ok, prob_ok, pv_ok, O_ok = sem("score_ok"), sem("prob_ok"), sem("pv_ok"), sem("O_ok")
        Otr_ok, On_ok, OT_ps, OT_ok, y_ok = (sem(n) for n in ("Otr_ok", "On_ok", "OT_ps", "OT_ok", "y_ok"))
        xbias_ok, x1_ok, xn2_ok = (sem(n) for n in ("xbias_ok", "x1_ok", "xn2_ok"))
        tail_dma = sem("tail_dma")
        xn2T_ps, xn2T_ok, logit_ok, gap_ok, e2_ok, chosen_ok = (
            sem(n) for n in ("xn2T_ps", "xn2T_ok", "logit_ok", "gap_ok", "e2_ok", "chosen_ok"))
        pos_ok, slot_ok, dest_ok, pay_ok, sent = (sem(n) for n in ("pos_ok", "slot_ok", "dest_ok", "pay_ok", "sent"))
        w_in, xe_in = [sem(f"w_in{n}") for n in range(2)], [sem(f"xe_in{n}") for n in range(4)]
        xeT_ps, xeT_ok, h_ps, hA_ok, hV_ok, ye_ps, yb_ok, yg_ok, added = (
            sem(n) for n in ("xeT_ps", "xeT_ok", "h_ps", "hA_ok", "hV_ok", "ye_ps", "yb_ok", "yg_ok", "added"))
        dve_chain, pool_chain = sem("dve_chain"), sem("pool_chain")
        dve_passed, pool_passed = sem("dve_passed"), sem("pool_passed")

        def steps(engine, run, count=None):
            rounds = (LAST - FIRST + 1) // 2
            for s in range(-3, FIRST):
                run(s, s)
            before_loop = count.value if count else 0
            with engine.Fori(0, rounds) as i:
                round_of[0] = i
                if count:
                    count.offset = i * count.per_round
                for j in range(2):
                    run(FIRST + 2 * i + j, FIRST + j)
            round_of[0] = 0
            if count:
                assert count.value - before_loop == count.per_round, count.value - before_loop
                count.offset, count.value = 0, before_loop + rounds * count.per_round
            for s in range(LAST + 1, BATCHES + 1):
                run(s, s)

        def live(like, b):
            return 0 <= like + b < BATCHES

        round_of = [0]

        def pair(s, k, b):
            return (k + b) // 2 + 1 + round_of[0]

        def atleast(engine, semaphore, value, like):
            assert like or isinstance(round_of[0], int)
            if like > 0:
                engine.wait_ge(semaphore, value)

        def apart(engine, passed):
            if not isinstance(round_of[0], int):
                engine.sem_inc(passed, 1)

        free_from_start = {"pe": (Otr_ok, OT_ps), "dve": (x1_ok, slot_ok), "pool": (xbias_ok, dest_ok, pay_ok)}

        block = ctx.enter_context(nc.Block())

        @block.sync
        def _(sp):
            def x_rows(b):
                return x[bass.ds(b * T, T), :].rearrange("(t p) d -> p t d", p=128)

            sp.dma_start(xin[:, 0], x_rows(0)).then_inc(x_in[0], 16)
            sp.dma_start(C[:], cst).then_inc(cst_in, 16)
            sp.dma_start(W[:], wts).then_inc(wts_in, 16)
            sp.dma_start(bo_all[:], bo.partition_broadcast(128)).then_inc(bo_in, 16)
            sp.wait_ge(ones_set, 1)
            for p in range(2):
                sp.dma_start(QK[p][PART_ROWS:SCORE_ROWS, :, 1].bitcast(fp32), ones[:]).then_inc(ones_in, 16)

            def load_expert(e, j):
                sp.dma_start(w1s[:, j], w1[bass.ds(e * D, D), :]).then_inc(w_in[j], 16)
                sp.dma_start(w2s[:, j], w2[bass.ds(e * HIDDEN, HIDDEN), :].rearrange("(c p) d -> p c d", p=128)
                             ).then_inc(w_in[j], 16)
                sp.dma_start(b1s[:, j], b1[bass.ds(e * 128, 128), :]).then_inc(w_in[j], 16)
                sp.dma_start(b2s[:, j], b2[bass.ds(e, 1), :].rearrange("a d -> (a d)").partition_broadcast(128)
                             ).then_inc(w_in[j], 16)

            def run(s, k):
                def move(half, b, kb):
                    p = kb % 2
                    atleast(sp, score_ok, (b - 2) * HEADS + (half + 1) * HALF, kb - 1)
                    sp.wait_ge(parts_ok, b + 1)
                    a, z = 64 * half, 64 * half + 64
                    for n, (lo, st) in enumerate([(0, 2), (0, 3), (1, 1)]):
                        sp.dma_start(QK[p][n * HD:(n + 1) * HD, half * HALF:(half + 1) * HALF].bitcast(fp32),
                                     parts[a:z, p, lo:lo + st + 1:st, :].bitcast(fp32)).then_inc(moved[half], 16)

                def move_max(half, b, kb):
                    p = kb % 2
                    sp.wait_ge(mT_ok, 2 * b + half + 1)
                    sp.dma_start(QK[p][PART_ROWS:SCORE_ROWS, half * HALF:(half + 1) * HALF, 0].bitcast(fp32),
                                 mT[:, half].bitcast(fp32)).then_inc(max_in[half], 16)

                if 1 <= k + 3 < BATCHES:
                    atleast(sp, xn1_ok, s + 2, k + 2)
                    sp.dma_start(xin[:, (k + 3) % 2], x_rows(s + 3)).then_inc(x_in[(k + 3) % 2], 16)
                if live(k, -1):
                    sp.wait_ge(xbias_ok, s)
                    sp.dma_start(xres[:], x_rows(s - 1)).then_inc(tail_dma, 16)
                if live(k, 1):
                    move(1, s + 1, k + 1)
                if live(k, 0):
                    move_max(1, s, k)
                if live(k, 1):
                    move_max(0, s + 1, k + 1)
                if live(k, -1):
                    sp.wait_ge(x1_ok, s + 1)
                    sp.dma_start(out[bass.ds((s - 1) * T, T), :].rearrange("(t p) d -> p t d", p=128),
                                 x1[:]).then_inc(tail_dma, 16)
                if live(k, 2):
                    move(0, s + 2, k + 2)
                if k == BATCHES - 2:
                    for e in range(2):
                        load_expert(e, e)

            steps(sp, run)
            sp.wait_ge(sent, 16 + 16 * TILES * TOPK * BATCHES)

            def load_rows(e, p):
                sp.dma_start(xe[:, p], rows[bass.ds(e * CAPACITY, CAPACITY), :].rearrange("(t p) r -> p t r", p=128)
                             ).then_inc(xe_in[p], 16)

            for e in range(4):
                load_rows(e, e)

            def refill(e):
                sp.wait_ge(ye_ps, e + 1)
                sp.wait_ge(yb_ok, e + 1)
                load_expert(e + 2, e % 2)

            for e in range(EXPERTS - 2):
                refill(e)
                if e < EXPERTS - 4:
                    sp.wait_ge(added, 16 * SLOT_TILES * (e + 1))
                    load_rows(e + 4, e)
            sp.wait_ge(added, 16 * SLOT_TILES * EXPERTS)

        @block.tensor
        def _(pe):
            mm, tr = nc.tensor.matmul, nc.tensor.transpose
            for free in free_from_start["pe"]:
                pe.sem_inc(free, 1)
            pe.wait_ge(wts_in, 16)
            pe.wait_ge(bv_ok, 1)
            mm(psC[:, 0:D], bv_rep[:], W[:, W_O:W_O + D], start=True, stop=True).then_inc(bias_ps, 1)
            pe.wait_ge(cst_in, 16)

            def run(s, k):
                p = k % 2

                def x_transpose():
                    pe.wait_ge(xn1_ok, s + 3)
                    atleast(pe, mT_ok, 2 * s + 1, k + 1)
                    for t in range(TILES):
                        i = tr(psB[:, 128 * t:128 * t + 128], xn1[:, p, t], ident)
                    i.then_inc(xT_ps, 1)

                def project(ps, cols, wait_bank, done):
                    pe.wait_ge(xT_ok, s + 3)
                    wait_bank()
                    for n, c in enumerate(cols):
                        i = mm(ps[:, T * n:T * n + T], W[:, c:c + 128], xT[:, p], start=True, stop=True)
                    i.then_inc(done, 1)

                def project_v():
                    if live(k, 2):
                        pe.wait_ge(qk_ev, s + 3)
                    for t in range(TILES):
                        i = mm(psB[:, 128 * t:128 * t + 128], xT[:, 1 - p, 128 * t:128 * t + 128],
                               W[:, W_V:W_V + 128], start=True, stop=True)
                    i.then_inc(v_ps, 1)

                def max_transpose(half, b, kb, ps):
                    pe.wait_ge(mparts_ok, 2 * b + half + 1)
                    for t in range(TILES):
                        i = tr(ps[0:2 * HALF, 128 * t:128 * t + 128],
                               mparts[:, half, t].rearrange("p a h -> p (a h)").bitcast(fp32), ident)
                    i.then_inc(mT_ps, 1)

                def max_scores(h):
                    g = (s + 1) * HEADS + h
                    if h % HALF == 0:
                        pe.wait_ge(moved[h // HALF], 48 * (s + 2))
                    atleast(pe, max_ok, g - 1, (k + 1) * HEADS + h - 1)
                    for t in range(TILES):
                        i = mm(max_ps[h % 2][:, T * t:T * t + T], QK[1 - p][0:PART_ROWS, h, 0, 128 * t:128 * t + 128],
                               QK[1 - p][0:PART_ROWS, h, 1, :], start=True, stop=True)
                    i.then_inc(max_ps_ok, 1)

                def scores(h):
                    g = s * HEADS + h
                    if h % HALF == 0:
                        pe.wait_ge(max_in[h // HALF], 16 * (s + 1))
                    atleast(pe, prob_ok, g - 1, k * HEADS + h - 1)
                    for t in range(TILES):
                        i = mm(score_ps[h % 2][:, T * t:T * t + T], QK[p][0:SCORE_ROWS, h, 1, 128 * t:128 * t + 128],
                               QK[p][0:SCORE_ROWS, h, 0, :], start=True, stop=True)
                    i.then_inc(score_ok, 1)

                def values(b, kb, n):
                    grp, pos = n // 2, n % 2
                    pe.wait_ge(prob_ok, b * HEADS + 4 * n + 4)
                    if n == 0:
                        pe.wait_ge(v_ok, b + 1)
                        atleast(pe, O_ok, b, kb)
                    for t in range(TILES):
                        c = V_BASE[2 * t + pos] + 128 * grp
                        for j in range(4):
                            i = mm(pv_ps[32 * j:32 * j + 32, T * grp:T * grp + T],
                                   VA[:, kb % 2, c + 32 * j:c + 32 * j + 32],
                                   P[:, (4 * n + j) % 8, T * t:T * t + T],
                                   start=(pos == 0 and t == 0), stop=(pos == 1 and t == 1))
                    i.then_inc(pv_ok, 1)

                def o_transpose():
                    pe.wait_ge(O_ok, s)
                    pe.wait_ge(slot_ok, s)
                    for t in range(TILES):
                        for g in range(2):
                            i = tr(psC[:, 256 * t + 128 * g:256 * t + 128 * g + 128],
                                   O[:, g, 128 * t:128 * t + 128], ident)
                    i.then_inc(Otr_ok, 1)

                def on_transpose():
                    pe.wait_ge(On_ok, s)
                    for t in range(TILES):
                        i = tr(psC[:, 128 * t:128 * t + 128], On[:, t], ident)
                    i.then_inc(OT_ps, 1)

                def project_out():
                    pe.wait_ge(OT_ok, s)
                    for t in range(TILES):
                        i = mm(psC[:, 128 * t:128 * t + 128], OT[:, 128 * t:128 * t + 128], W[:, W_O:W_O + D],
                               start=True, stop=True)
                    i.then_inc(y_ok, 1)

                def xn2_transpose():
                    pe.wait_ge(xn2_ok, s)
                    for t in range(TILES):
                        i = tr(psC[:, 128 * t:128 * t + 128], pay[:, 1 - p, 0, t, 0:D], ident)
                    i.then_inc(xn2T_ps, 1)

                def router():
                    pe.wait_ge(xn2T_ok, s)
                    for t in range(TILES):
                        i = mm(psC[:, EXPERTS * t:EXPERTS * t + EXPERTS], xn2T[:, 128 * t:128 * t + 128],
                               W[:, W_R:W_R + EXPERTS], start=True, stop=True)
                    i.then_inc(logit_ok, 1)

                def positions():
                    pe.wait_ge(chosen_ok, s)
                    mm(psC[:, 64:64 + TILES * EXPERTS], before[:], chosen[:].rearrange("p t e -> p (t e)"),
                       start=True, stop=False)
                    mm(psC[:, 64:64 + TILES * EXPERTS], every[:], seen[:, 0:TILES].rearrange("p t e -> p (t e)"),
                       start=False, stop=True).then_inc(pos_ok, 1)

                for h in range(HEADS):
                    if live(k, 0):
                        scores(h)
                    if live(k, 1):
                        max_scores(h)
                    if k == 0 and h == 0:
                        pe.wait_ge(ones_in, 32)
                        pe.wait_ge(attn_bias_ok, 1)
                        pe.wait_ge(before_ok, 1)
                    if h == 0 and live(k, 2):
                        x_transpose()
                    if h == 1 and live(k, -1):
                        values(s - 1, k - 1, 3)
                    if h == 1 and live(k, 0):
                        max_transpose(1, s, k, psA)
                    if h == 2 and live(k, 2):
                        project(psB, (W_Q, W_K), lambda: None, qk_ps)
                    if h == 3 and live(k, 2):
                        project(psA, (W_QS, W_KS), lambda: atleast(pe, mT_ok, 2 * s + 2, k + 1), qs_ps)
                    if h == 3 and live(k, -1):
                        o_transpose()
                    if h == 5 and live(k, 0):
                        values(s, k, 0)
                    if h == 5 and live(k, -1):
                        on_transpose()
                    if h == 7 and live(k, 1):
                        project_v()
                    if h == 7 and live(k, -1):
                        project_out()
                    if h == 9 and live(k, 0):
                        values(s, k, 1)
                    if h == 10 and live(k, 1):
                        pe.wait_ge(v_ok, s + 2)
                        max_transpose(0, s + 1, k + 1, psB)
                    if h == 11 and live(k, -1):
                        xn2_transpose()
                    if h == 13 and live(k, 0):
                        values(s, k, 2)
                    if h == 12 and live(k, -1):
                        router()
                    if h == 14 and live(k, -1):
                        positions()

            steps(pe, run)

            pe.wait_ge(prob_ok, BATCHES * HEADS)
            pe.wait_ge(max_ok, BATCHES * HEADS)
            pe.wait_ge(mT_ok, 2 * BATCHES)
            pe.wait_ge(O_ok, BATCHES)

            def gather(e, r, q):
                pe.wait_ge(xe_in[q], 16 * (r + 1))
                pe.wait_ge(xeT_ok, e)
                for t in range(SLOT_TILES):
                    last = tr(bank[4][:, 128 * t:128 * t + 128], xe[:, q, t, 0:D], ident)
                last.then_inc(xeT_ps, 1)

            def expert(e, r, q, after):
                j = q % 2
                pe.wait_ge(w_in[j], 64 * (2 * r + q // 2 + 1))
                pe.wait_ge(xeT_ok, e + 1)
                for c in range(CHUNKS):
                    mm(bank[c][:, 0:CAPACITY], w1s[:, j, 128 * c:128 * c + 128], xeT[:, j], start=True, stop=True
                       ).then_inc(h_ps, 1)
                if after:
                    gather(e + 1, r + (q + 1) // 4, (q + 1) % 4)
                pe.wait_ge(yb_ok, e)
                for t in range(SLOT_TILES):
                    for c in range(CHUNKS):
                        if t == 0:
                            pe.wait_ge(hV_ok if c % 2 else hA_ok, 2 * e + c // 2 + 1)
                        last = mm(bank[5][:, 128 * t:128 * t + 128], hT[:, c, 128 * t:128 * t + 128],
                                  w2s[:, j, c], start=(c == 0), stop=(c == CHUNKS - 1))
                last.then_inc(ye_ps, 1)

            gather(0, 0, 0)
            for r in range(EXPERTS // 4):
                for q in range(4):
                    expert(4 * r + q, r, q, 4 * r + q < EXPERTS - 1)

        @block.scalar
        def _(act):
            fn = nc.scalar.activation
            act.wait_ge(wts_in, 16)
            act.wait_ge(va_set, 1)

            def run(s, k):
                p = k % 2

                def probs(h):
                    g = s * HEADS + h
                    act.wait_ge(score_ok, g + 1)
                    if h % 4 == 0:
                        atleast(act, pv_ok, 4 * s + h // 4 - 1, 4 * k + h // 4 - 1)
                    fn(P[:, h % 8], score_ps[h % 2][:], ACT.Exp, scale=float(HD) ** -0.5).then_inc(prob_ok, 1)

                def copy_max(half, b, ps):
                    act.wait_ge(mT_ps, 2 * b + half + 1)
                    atleast(act, max_in[half], 16 * b, k + 1 - half)
                    fn(mT[:, half], ps[0:2 * HALF, 0:T], ACT.Copy).then_inc(mT_ok, 1)

                def copy_x():
                    act.wait_ge(xT_ps, s + 3)
                    atleast(act, v_ps, s + 1, k + 1)
                    fn(xT[:, p], psB[:, 0:T], ACT.Copy).then_inc(xT_ok, 1)

                def copy_v():
                    act.wait_ge(v_ps, s + 2)
                    atleast(act, pv_ok, 4 * s, k)
                    v = VA[:, 1 - p].rearrange("p (i r) -> p i r", r=V_STEP)[:, :, 0:256]
                    fn(v.rearrange("p i (g c) -> p i g c", c=32)[:, :, :, 0:HD],
                       psB[:, 0:2 * 128].rearrange("p (i g c) -> p i g c", i=4, c=HD), ACT.Copy).then_inc(v_ok, 1)

                def copy_o():
                    act.wait_ge(pv_ok, 4 * s)
                    act.wait_ge(Otr_ok, s)
                    fn(O[:].rearrange("p g t -> p (g t)"), pv_ps[:], ACT.Copy).then_inc(O_ok, 1)

                def copy_on():
                    act.wait_ge(OT_ps, s + 1)
                    fn(OT[:], psC[:, 0:T], ACT.Copy).then_inc(OT_ok, 1)

                def copy_xn2():
                    act.wait_ge(xn2T_ps, s)
                    fn(xn2T[:], psC[:, 0:T], ACT.Copy).then_inc(xn2T_ok, 1)

                def exp_gap():
                    act.wait_ge(gap_ok, s)
                    fn(e2[:], gap[:], ACT.Exp).then_inc(e2_ok, 1)

                for h in range(HEADS):
                    if live(k, 0):
                        probs(h)
                    if h == 1 and live(k, 2):
                        copy_x()
                    if h == 2 and live(k, -1):
                        copy_o()
                    if h == 2 and live(k, 0):
                        copy_max(1, s, psA)
                    if h == 6 and live(k, -1):
                        copy_on()
                    if h == 8 and live(k, 1):
                        copy_v()
                    if h == 11 and live(k, 1):
                        copy_max(0, s + 1, psB)
                    if h == 12 and live(k, -1):
                        copy_xn2()
                    if h == 14 and live(k, -1):
                        exp_gap()

            steps(act, run)

            def expert(e, j):
                act.wait_ge(xeT_ps, e + 1)
                fn(xeT[:, j], bank[4][:, 0:CAPACITY], ACT.Copy).then_inc(xeT_ok, 1)
                for c in (0, 2):
                    act.wait_ge(h_ps, 4 * e + c + 1)
                    act.wait_ge(ye_ps, e)
                    fn(hT[:, c], bank[c][:, 0:CAPACITY], ACT.Relu, bias=b1s[:, j, c:c + 1]).then_inc(hA_ok, 1)

            for e in range(EXPERTS):
                expert(e, e % 2)

        @block.vector
        def _(dve):
            V = nc.vector
            count = Count(DVE_LINKS)

            def link(ins, alone=False):
                ins.then_inc(dve_chain, 1)
                dve.wait_ge(dve_chain, count.next())
                if alone:
                    apart(dve, dve_passed)

            for free in free_from_start["dve"]:
                dve.sem_inc(free, 1)
            V.memset(ones[:], 1.0).then_inc(ones_set, 1)
            link(V.memset(VA[:], 0.0))
            for p in range(2):
                for n in range(4):
                    c = V_BASE[n] + 9 * (n % 2) + HD
                    i = V.memset(VA[:, p, c:c + 32 * 7 + 1:32], 1.0)
            i.then_inc(va_set, 1)
            V.memset(seen[:], 0.0)

            def first_constants():
                dve.wait_ge(wts_in, 16)
                V.tensor_copy(bv_rep[:], W[:, W_BV:W_BV + 1].to_broadcast([128, 128])).then_inc(bv_ok, 1)
                V.memset(every[:], 1.0)
                V.tensor_copy(before[:], C[:, C_UP:C_UP + 128]).then_inc(before_ok, 1)

            def second_constants():
                dve.wait_ge(bias_ps, 1)
                dve.wait_ge(bo_in, 16)
                V.tensor_tensor(attn_bias[:], psC[:, 0:D], bo_all[:], ALU.add).then_inc(attn_bias_ok, 1)

            def run(s, k):
                p = k % 2

                def reduce(h):
                    g = (s + 1) * HEADS + h
                    dve.wait_ge(max_ps_ok, g + 1)
                    V.tensor_reduce(negmax[:, h // HALF, :, h % HALF],
                                    max_ps[h % 2][:].rearrange("p (t k) -> p t k", t=TILES),
                                    axis=AX.X, op=ALU.max, negate=True).then_inc(max_ok, 1)

                def split_max(half):
                    dve.wait_ge(max_ok, (s + 1) * HEADS + (half + 1) * HALF)
                    atleast(dve, mT_ps, 2 * (s + 1) + half - 1, k + 1)
                    link(V.tensor_copy(mparts[:, half, :, 0], negmax[:, half]))
                    V.tensor_tensor(mparts[:, half, :, 1], negmax[:, half], mparts[:, half, :, 0].bitcast(fp32),
                                    ALU.subtract).then_inc(mparts_ok, 1)

                def norm1_stats():
                    b = (k + 3) % 2
                    dve.wait_ge(x_in[b], 16 * pair(s, k, 3))
                    atleast(dve, xn1_ok, s + 2, k + 2)
                    for t in range(TILES):
                        i = V.bn_stats(stats1[:, b, t], xin[:, b, t])
                    link(i, True)
                    for t in range(TILES):
                        i = V.bn_aggr(mv1[:, b, t], stats1[:, b, t])
                    i.then_inc(stats1_ok, 1)

                def rotate(ps, ready, first, table, into, done):
                    dve.wait_ge(ready, s + 3)
                    atleast(dve, rope_ok, s + 2, k + 2)
                    for n in range(2):
                        i = V.scalar_tensor_tensor(
                            out=into[:, n], in0=ps[:, T * n:T * n + T],
                            scalar=W[:, W_BIAS + first + n:W_BIAS + first + n + 1], in1=C[:, table:table + T],
                            op0=ALU.add, op1=ALU.mult)
                    i.then_inc(done, 1)

                def normalise():
                    dve.wait_ge(Otr_ok, s + 1)
                    o = psC[:].rearrange("p (a c) -> p a c", c=32)[:, :, 0:18].rearrange("p a (b r) -> p a b r", r=9)
                    link(V.reciprocal(rsum[:].unsqueeze(3), o[:, :, :, HD:HD + 1]))
                    dve.wait_ge(OT_ps, s)
                    V.tensor_tensor(On[:].rearrange("p t (a b d) -> p (t a) b d", b=2, d=HD), o[:, :, :, 0:HD],
                                    rsum[:].unsqueeze(3).to_broadcast([128, TILES * 8, 2, HD]), ALU.mult
                                    ).then_inc(On_ok, 1)

                def residual():
                    dve.wait_ge(y_ok, s)
                    dve.wait_ge(xbias_ok, s + 1)
                    dve.wait_ge(tail_dma, 16 * (2 * s - 1))
                    dve.wait_ge(pay_ok, s)
                    link(V.tensor_tensor(x1[:], psC[:, 0:T].rearrange("p (t d) -> p t d", t=TILES), xbias[:], ALU.add))
                    for t in range(TILES):
                        i = V.bn_stats(stats2[:, t], x1[:, t])
                    link(i, True)
                    for t in range(TILES):
                        i = V.bn_aggr(mv2[:, t], stats2[:, t])
                    i.then_inc(x1_ok, 1)

                def choose():
                    dve.wait_ge(logit_ok, s)
                    dve.wait_ge(dest_ok, s)
                    apart(dve, dve_passed)
                    for t in range(TILES):
                        i = V.max(best[:, t], psC[:, EXPERTS * t:EXPERTS * t + EXPERTS])
                    link(i, True)
                    for t in range(TILES):
                        i = V.max_index(besti[:, t], best[:, t], psC[:, EXPERTS * t:EXPERTS * t + EXPERTS])
                    V.tensor_tensor(gap[:], best[:, :, 1], best[:, :, 0], ALU.subtract).then_inc(gap_ok, 1)
                    dve.wait_ge(gap_ok, s)
                    link(V.tensor_copy(choice[:], besti[:, :, 0:TOPK]))
                    link(V.tensor_tensor(
                        onehot[:], choice[:].unsqueeze(3).to_broadcast([128, TILES, TOPK, EXPERTS]),
                        C[:, C_IOTA:C_IOTA + TILES * TOPK * EXPERTS].rearrange("p (t k e) -> p t k e", t=TILES, k=TOPK),
                        ALU.is_equal))
                    link(V.tensor_tensor(chosen[:], onehot[:, :, 0], onehot[:, :, 1], ALU.add))
                    link(V.tensor_tensor(seen[:, 1], seen[:, 0], chosen[:, 0], ALU.add))
                    V.tensor_tensor(seen[:, 2], seen[:, 1], chosen[:, 1], ALU.add).then_inc(chosen_ok, 1)

                def place():
                    dve.wait_ge(pos_ok, s)
                    dve.wait_ge(e2_ok, s)
                    dve.wait_ge(pay_ok, s + 1)
                    for t in range(TILES):
                        i = V.tensor_tensor(
                            hit[:, t], onehot[:, t],
                            psC[:, 64 + EXPERTS * t:64 + EXPERTS * t + EXPERTS].unsqueeze(1).to_broadcast(
                                [128, TOPK, EXPERTS]), ALU.mult)
                    link(i)
                    V.tensor_reduce(slot[:], hit[:], axis=AX.X, op=ALU.add)
                    link(V.tensor_scalar(den[:], e2[:], 1.0, None, ALU.add))
                    link(V.reciprocal(pay[:, 1 - p, 0, :, D:D + 1], den[:].unsqueeze(2)))
                    V.tensor_tensor(pay[:, 1 - p, 1, :, D], pay[:, 1 - p, 0, :, D], e2[:], ALU.mult)
                    V.tensor_copy(seen[:, 0], seen[:, 2]).then_inc(slot_ok, 1)

                for h in range(HEADS):
                    if live(k, 1):
                        reduce(h)
                        if h % HALF == HALF - 1:
                            split_max(h // HALF)
                    if h == 5 and live(k, 3):
                        norm1_stats()
                        if k == -3:
                            first_constants()
                        if k == -2:
                            second_constants()
                    if h == 3 and live(k, 2):
                        rotate(psB, qk_ps, 0, C_COS, rot1, qk_ev)
                    if h == 4 and live(k, 2):
                        rotate(psA, qs_ps, 2, C_SIN, rot2, qs_ev)
                    if h == 4 and live(k, -1):
                        normalise()
                    if h == 8 and live(k, -1):
                        residual()
                    if h == 13 and live(k, -1):
                        choose()
                    if h == 15 and live(k, -1):
                        place()

            steps(dve, run, count)

            def expert(e, j):
                for c in (1, 3):
                    dve.wait_ge(h_ps, 4 * e + c + 1)
                    dve.wait_ge(ye_ps, e)
                    V.tensor_scalar(hT[:, c], bank[c][:, 0:CAPACITY], b1s[:, j, c:c + 1], 0.0, ALU.add, ALU.max
                                    ).then_inc(hV_ok, 1)
                dve.wait_ge(ye_ps, e + 1)
                dve.wait_ge(yg_ok, e)
                V.tensor_tensor(yb[:], bank[5][:, 0:CAPACITY].rearrange("p (t d) -> p t d", d=D),
                                b2s[:, j].unsqueeze(1).to_broadcast([128, SLOT_TILES, D]), ALU.add
                                ).then_inc(yb_ok, 1)

            for e in range(EXPERTS):
                expert(e, e % 2)

        @block.gpsimd
        def _(pool):
            G = nc.gpsimd
            count = Count(POOL_LINKS)

            def link(ins):
                ins.then_inc(pool_chain, 1)
                pool.wait_ge(pool_chain, count.next())
                apart(pool, pool_passed)

            for free in free_from_start["pool"]:
                pool.sem_inc(free, 1)
            link(G.memset(minus_half[:], -0.5))

            def inverse_deviation(mv, rstd, shift):
                link(G.tensor_scalar(rstd, mv[:, :, 1], 1.0, EPS, ALU.mult, ALU.add))
                link(G.tensor_tensor(rstd, rstd, minus_half[:], ALU.pow))
                link(G.tensor_tensor(shift, mv[:, :, 0], rstd, ALU.mult))
                link(G.tensor_scalar(shift, shift, -1.0, 0.0, ALU.mult, ALU.add))

            def run(s, k):
                p = k % 2

                def norm1():
                    b = (k + 3) % 2
                    pool.wait_ge(stats1_ok, s + 4)
                    atleast(pool, xT_ps, s + 2, k + 2)
                    apart(pool, pool_passed)
                    inverse_deviation(mv1[:, b], rstd1[:, b], shift1[:, b])
                    for t in range(TILES):
                        i = G.tensor_scalar(xn1[:, b, t], xin[:, b, t], rstd1[:, b, t:t + 1], shift1[:, b, t:t + 1],
                                            ALU.mult, ALU.add)
                    i.then_inc(xn1_ok, 1)

                def split_rope():
                    pool.wait_ge(qk_ev, s + 3)
                    pool.wait_ge(qs_ev, s + 3)
                    G.tensor_tensor(rope[:], rot1[:], rot2[:], ALU.add).then_inc(rope_ok, 1)
                    for half in range(2):
                        atleast(pool, moved[half], 48 * (s + 1), k + 1)
                    pool.wait_ge(rope_ok, s + 3)
                    apart(pool, pool_passed)
                    G.tensor_scalar(parts[:, p, 0:4:2], rope[:], 1.0, 0.0, ALU.mult, ALU.add).then_inc(hi_ok, 1)
                    pool.wait_ge(hi_ok, s + 3)
                    G.tensor_tensor(parts[:, p, 1:4:2], rope[:], parts[:, p, 0:4:2].bitcast(fp32), ALU.subtract
                                    ).then_inc(parts_ok, 1)

                def add_residual():
                    pool.wait_ge(tail_dma, 16 * (2 * s - 1))
                    pool.wait_ge(x1_ok, s)
                    if k == 1:
                        pool.wait_ge(attn_bias_ok, 1)
                    G.tensor_tensor(xbias[:], xres[:], attn_bias[:].unsqueeze(1).to_broadcast([128, TILES, D]), ALU.add
                                    ).then_inc(xbias_ok, 1)

                def norm2():
                    pool.wait_ge(x1_ok, s + 1)
                    pool.wait_ge(sent, 16 + 16 * TILES * TOPK * (s - 1))
                    apart(pool, pool_passed)
                    inverse_deviation(mv2[:], rstd2[:], shift2[:])
                    for c in range(TOPK):
                        for t in range(TILES):
                            i = G.tensor_scalar(pay[:, 1 - p, c, t, 0:D], x1[:, t], rstd2[:, t:t + 1],
                                                shift2[:, t:t + 1], ALU.mult, ALU.add)
                        if c == 0:
                            i.then_inc(xn2_ok, 1)
                    link(G.tensor_copy(pay[:, 1 - p, :, :, D + 1].bitcast(i32), tok[:].unsqueeze(1).to_broadcast(
                        [128, TOPK, TILES])))
                    G.tensor_scalar(tok[:], tok[:], 1.0, float(T), ALU.mult, ALU.add).then_inc(pay_ok, 1)

                def dispatch():
                    pool.wait_ge(slot_ok, s + 1)
                    apart(pool, pool_passed)
                    link(G.tensor_scalar(over[:], slot[:], float(CAPACITY), float(NOWHERE), ALU.is_ge, ALU.mult))
                    link(G.tensor_scalar(base[:], choice[:], float(CAPACITY), 0.0, ALU.mult, ALU.add))
                    link(G.tensor_tensor(base[:], base[:], over[:], ALU.add))
                    link(G.tensor_tensor(base[:], base[:], slot[:], ALU.add))
                    G.tensor_scalar(dest[:, 1 - p], base[:], 1.0, 0.0, ALU.mult, ALU.add).then_inc(dest_ok, 1)
                    pool.wait_ge(dest_ok, s + 1)
                    apart(pool, pool_passed)
                    for t in range(TILES):
                        for c in range(TOPK):
                            G.indirect_dma_start(
                                out=rows, out_offset=bass.IndirectOffsetOnAxis(ap=dest[:, 1 - p, t, c:c + 1], axis=0),
                                in_=pay[:, 1 - p, c, t], in_offset=None, bounds_check=SLOTS - 1, oob_is_err=False,
                            ).then_inc(sent, 16)

                if live(k, -1):
                    add_residual()
                if live(k, 2):
                    split_rope()
                if live(k, -1):
                    norm2()
                if live(k, 3):
                    norm1()
                if live(k, -1):
                    dispatch()
                if k == -3:
                    link(G.memset(blank[:], 0.0))
                    G.memset(blank[:, :, D + 1:D + 2].bitcast(i32), NOWHERE).then_inc(blank_set, 1)
                    pool.wait_ge(blank_set, 1)
                    G.dma_start(rows.rearrange("(p n) r -> p n r", p=128), blank[:]).then_inc(sent, 16)
                    pool.wait_ge(cst_in, 16)
                    link(G.tensor_copy(tok[:], C[:, C_TOK:C_TOK + TILES]))

            steps(pool, run, count)
            pool.wait_ge(tail_dma, 16 * 2 * BATCHES)

            def expert(e, q):
                pool.wait_ge(yb_ok, e + 1)
                G.tensor_tensor(yg[:, q % 2], yb[:], xe[:, q, :, D:D + 1].to_broadcast([128, SLOT_TILES, D]), ALU.mult
                                ).then_inc(yg_ok, 1)
                pool.wait_ge(yg_ok, e + 1)
                atleast(pool, added, 16 * SLOT_TILES * e, e)
                for t in range(SLOT_TILES):
                    G.indirect_dma_start(
                        out=out, out_offset=bass.IndirectOffsetOnAxis(ap=xe[:, q, t, D + 1:D + 2].bitcast(i32), axis=0),
                        in_=yg[:, q % 2, t], in_offset=None, bounds_check=TOKENS - 1, oob_is_err=False,
                        compute_op=ALU.add).then_inc(added, 16)

            for e in range(EXPERTS):
                expert(e, e % 4)


def kernel(**inputs):
    import numpy as np
    import concourse.bacc as bacc
    from concourse.bass_utils import run_bass_kernel_spmd

    f = {n: np.asarray(a) for n, a in inputs.items()}
    qk = np.arange(D).reshape(2, HALF, HD).transpose(0, 2, 1).ravel()
    swapped = np.arange(D).reshape(2, HALF, HD)[:, :, np.arange(HD) ^ 1].transpose(0, 2, 1).ravel()
    vcols = np.arange(D).reshape(2, 2, 4, HD).transpose(1, 0, 2, 3).ravel()
    orows = np.arange(D).reshape(2, 2, 4, HD).transpose(0, 2, 1, 3).ravel()
    p = "L0_attn_"
    wq, wk, wv, wo = (f[p + n] for n in ("Wq", "Wk", "Wv", "Wo"))
    bq, bk, bv = (f[p + n] for n in ("bq", "bk", "bv"))
    wts = np.concatenate([
        wq[qk].T, wk[qk].T, wq[swapped].T, wk[swapped].T, wv[vcols].T, wo[:, orows].T, f["L0_ffn_w_router"],
        bq[qk][:, None], bk[qk][:, None], bq[swapped][:, None], bk[swapped][:, None], bv[orows][:, None]], axis=1)

    freq = (np.float32(1) / np.float32(10000) ** (np.arange(0, HD, 2, dtype=np.float32) / np.float32(HD)))
    angle = np.repeat(np.arange(T, dtype=np.float32)[:, None] * freq[None, :], 2, axis=-1).astype(np.float32)
    cos, sin = np.cos(angle), np.sin(angle) * np.where(np.arange(HD) % 2 == 0, -1, 1).astype(np.float32)
    row_feature = np.tile(np.repeat(np.arange(HD), HALF), 2)
    part = np.arange(128)
    cst = np.concatenate([
        np.eye(128), cos.T[row_feature], sin.T[row_feature], part[:, None] < part[None, :],
        np.tile(np.arange(EXPERTS), (128, TILES * TOPK)), part[:, None] + 128 * np.arange(TILES)[None, :],
    ], axis=1).astype(np.float32)

    arrays = {
        "x": f[p + "x"].reshape(TOKENS, D), "wts": wts, "cst": cst, "bo": f[p + "bo"],
        "w1": f["L0_ffn_w1"].reshape(EXPERTS * D, HIDDEN),
        "b1": f["L0_ffn_b1"].reshape(EXPERTS, CHUNKS, 128).transpose(0, 2, 1).reshape(EXPERTS * 128, CHUNKS),
        "w2": f["L0_ffn_w2"].reshape(EXPERTS * HIDDEN, D), "b2": f["L0_ffn_b2"],
    }
    arrays = {n: np.ascontiguousarray(a) for n, a in arrays.items()}
    nc = bacc.Bacc("TRN2", target_bir_lowering=False, num_devices=1)
    args = {n: nc.dram_tensor(n, a.shape, mybir.dt.from_np(a.dtype), kind="ExternalInput").ap()
            for n, a in arrays.items()}
    out = nc.dram_tensor("out", (TOKENS, D), mybir.dt.float32, kind="ExternalOutput").ap()
    rows = nc.dram_tensor("rows", (SLOTS, ROW), mybir.dt.float32, kind="Internal").ap()
    build(nc, **args, out=out, rows=rows)
    r = run_bass_kernel_spmd(nc, [arrays], core_ids=[0])
    return r.results[0]["out"].reshape(BATCHES, T, D)
```

```python
import concourse.bass as bass
from concourse import mybir
from contextlib import ExitStack

BATCHES, T, D = 8, 256, 128
HEADS, HD = 16, 8
TILES = T // 128
TOKENS = BATCHES * T
EXPERTS, HIDDEN, TOPK = 8, 512, 2
CAPACITY = int(1.5 * 4 * 256 * TOPK / EXPERTS)
SLOT_TILES = CAPACITY // 128
CHUNKS = HIDDEN // 128
SLOTS = EXPERTS * CAPACITY
ROW = D + 2
NOWHERE = 1 << 20
EPS = 1e-5
HALF = HEADS // 2

PART_ROWS = 96
SCORE_ROWS = PART_ROWS + 2

W_Q, W_K, W_QS, W_KS, W_V, W_O, W_R = 0, 128, 256, 384, 512, 640, 768
W_BIAS = W_R + EXPERTS
W_BV = W_BIAS + 4
W_COLS = W_BV + 1
C_ID, C_COS, C_SIN, C_UP, C_IOTA = 0, 128, 128 + T, 128 + 2 * T, 256 + 2 * T
C_TOK = C_IOTA + TILES * TOPK * EXPERTS
C_COLS = C_TOK + TILES

V_STEP = 265
V_BASE = [V_STEP * i - 9 * (i % 2) for i in range(4)]
V_COLS = 4 * V_STEP

FIRST, LAST = 1, 4
LOGITS, POS = 256, 320
XT_H = 1
SEAM = 8
DVE_LINKS, POOL_LINKS = 28, 6


class Count:

    def __init__(self, per_round):
        self.value, self.offset, self.per_round = 0, 0, per_round

    def in_loop(self):
        return not isinstance(self.offset, int)

    def next(self):
        self.value += 1
        return self.value + self.offset


def build(nc, x, wts, cst, bo, w1, b1, w2, b2, out, rows):
    fp32, fp32r, bf16 = mybir.dt.float32, mybir.dt.float32r, mybir.dt.bfloat16
    i32, u32 = mybir.dt.int32, mybir.dt.uint32
    ALU, ACT, AX = mybir.AluOpType, mybir.ActivationFunctionType, mybir.AxisListType
    ctx = ExitStack()
    with ctx:
        def sb(name, shape, dt=fp32):
            return ctx.enter_context(nc.sbuf_tensor(name, shape, dt))

        def sem(name):
            return ctx.enter_context(nc.semaphore(name))

        bank = [ctx.enter_context(nc.psum_tensor(f"bank{i}", [128, 512], fp32)) for i in range(8)]
        score_ps, max_ps, pv_ps = bank[0:2], bank[2:4], bank[4]
        psA, psB, psC = bank[5], bank[6], bank[7]

        W = sb("W", [128, W_COLS])
        C = sb("C", [128, C_COLS])
        bo_all = sb("bo_all", [128, D])
        ones = sb("ones", [2 * HEADS, T])
        bv_rep = sb("bv_rep", [128, 128])
        attn_bias = sb("attn_bias", [128, D])
        before = sb("before", [128, 128], bf16)
        every = sb("every", [128, 128], bf16)
        minus_half = sb("minus_half", [128, TILES])
        blank = sb("blank", [128, SLOTS // 256, ROW])
        ident = C[:, C_ID:C_ID + 128]

        def logits(t):
            return psC[:, LOGITS + EXPERTS * t:LOGITS + EXPERTS * t + EXPERTS]


        xin = sb("xin", [128, 2, TILES, D])
        stats1 = sb("stats1", [128, 2, TILES, 6])
        mv1 = sb("mv1", [128, 2, TILES, 2])
        rstd1 = sb("rstd1", [128, 2, TILES])
        xn1 = sb("xn1", [128, 2, TILES, D])
        xT = sb("xT", [128, 2, T])
        rot1 = sb("rot1", [128, 2, T])
        rot2 = sb("rot2", [128, 2, T])
        rope = sb("rope", [128, 2, T])
        parts = sb("parts", [128, 2, 4, T], fp32r)
        QK = [sb(f"QK{p}", [SCORE_ROWS, HEADS, 2, T], fp32r) for p in range(2)]
        VA = sb("VA", [128, 2, V_COLS])
        negmax = sb("negmax", [128, 2, TILES, HALF])
        mparts = sb("mparts", [128, 2, TILES, 2, HALF], fp32r)
        mT = sb("mT", [2 * HALF, 2, T], fp32r)
        P = sb("P", [128, 8, 2 * T])
        O = sb("O", [128, 2, T])
        rsum = sb("rsum", [128, TILES * 8, 2])
        On = sb("On", [128, TILES, D])
        OT = sb("OT", [128, T])
        xres = sb("xres", [128, TILES, D])
        xbias = sb("xbias", [128, TILES, D])
        x1 = sb("x1", [128, TILES, D])
        stats2 = sb("stats2", [128, TILES, 6])
        mv2 = sb("mv2", [128, TILES, 2])
        rstd2 = sb("rstd2", [128, TILES])
        pay = sb("pay", [128, 2, TOPK, TILES, ROW])
        xn2T = sb("xn2T", [128, T])
        best = sb("best", [128, TILES, 8])
        besti = sb("besti", [128, TILES, 8], u32)
        choice = sb("choice", [128, TILES, TOPK])
        gap = sb("gap", [128, TILES])
        e2 = sb("e2", [128, TILES])
        den = sb("den", [128, TILES])
        onehot = sb("onehot", [128, TILES, TOPK, EXPERTS])
        chosen = sb("chosen", [128, TILES, EXPERTS], bf16)
        seen = sb("seen", [128, TILES + 1, EXPERTS], bf16)
        hit = sb("hit", [128, TILES, TOPK, EXPERTS])
        slot = sb("slot", [128, TILES, TOPK])
        over = sb("over", [128, TILES, TOPK])
        base = sb("base", [128, TILES, TOPK])
        dest = sb("dest", [128, 2, TILES, TOPK], i32)
        tok = sb("tok", [128, TILES])

        w1s = sb("w1s", [128, 2, HIDDEN])
        w2s = sb("w2s", [128, 2, CHUNKS, D])
        xe = sb("xe", [128, 4, SLOT_TILES, ROW])
        b1s = sb("b1s", [128, 2, CHUNKS])
        b2s = sb("b2s", [128, 2, D])
        xeT = sb("xeT", [128, 2, CAPACITY])
        hT = sb("hT", [128, CHUNKS, CAPACITY])
        yb = sb("yb", [128, SLOT_TILES, D])
        yg = sb("yg", [128, 2, SLOT_TILES, D])

        wts_in, cst_in, bo_in = sem("wts_in"), sem("cst_in"), sem("bo_in")
        bias_ps, attn_bias_ok, bv_ok, before_ok, va_set, ones_set, ones_in = (
            sem(n) for n in ("bias_ps", "attn_bias_ok", "bv_ok", "before_ok", "va_set", "ones_set", "ones_in"))
        blank_set = sem("blank_set")
        zero_ok = [sem("zero_ok0"), sem("zero_ok1")]
        x_in = [sem("x_in0"), sem("x_in1")]
        stats1_ok, xn1_ok = sem("stats1_ok"), sem("xn1_ok")
        xT_ps, xT_ok, qk_ps, qs_ps, qk_ev, qs_ev = (sem(n) for n in ("xT_ps", "xT_ok", "qk_ps", "qs_ps", "qk_ev", "qs_ev"))
        v_ps, v_ok, rope_ok, hi_ok, parts_ok = (sem(n) for n in ("v_ps", "v_ok", "rope_ok", "hi_ok", "parts_ok"))
        moved = [sem("moved0"), sem("moved1")]
        max_ps_ok, max_ok, mparts_ok, mT_ps, mT_ok = (sem(n) for n in ("max_ps_ok", "max_ok", "mparts_ok", "mT_ps", "mT_ok"))
        max_in = [sem("max_in0"), sem("max_in1")]
        score_ok, prob_ok, pv_ok, O_ok = sem("score_ok"), sem("prob_ok"), sem("pv_ok"), sem("O_ok")
        Otr_ok, On_ok, OT_ps, OT_ok, y_ok = (sem(n) for n in ("Otr_ok", "On_ok", "OT_ps", "OT_ok", "y_ok"))
        xbias_ok, x1_ok, rstd1_ok, rstd2_ok, xn2_ok = (
            sem(n) for n in ("xbias_ok", "x1_ok", "rstd1_ok", "rstd2_ok", "xn2_ok"))
        tail_dma = sem("tail_dma")
        xn2T_ps, xn2T_ok, logit_ok, gap_ok, e2_ok, chosen_ok = (
            sem(n) for n in ("xn2T_ps", "xn2T_ok", "logit_ok", "gap_ok", "e2_ok", "chosen_ok"))
        pos_ok, slot_ok, pay_ok, rows2_ok = (sem(n) for n in ("pos_ok", "slot_ok", "pay_ok", "rows2_ok"))
        sent = [sem("sent0"), sem("sent1")]
        w_in, xe_in = [sem(f"w_in{n}") for n in range(2)], [sem(f"xe_in{n}") for n in range(4)]
        xeT_ps, xeT_ok, h_ps, hA_ok, hV_ok, ye_ps, yb_ok, yg_ok, added = (
            sem(n) for n in ("xeT_ps", "xeT_ok", "h_ps", "hA_ok", "hV_ok", "ye_ps", "yb_ok", "yg_ok", "added"))
        dve_chain, pool_chain = sem("dve_chain"), sem("pool_chain")
        dve_passed, pool_passed = sem("dve_passed"), sem("pool_passed")

        def steps(engine, late, early, count=None):
            rounds = (LAST - FIRST + 1) // 2
            for s in range(-4, FIRST):
                late(s, s)
                early(s + 1, s + 1)
            before_loop = count.value if count else 0
            with engine.Fori(0, rounds) as i:
                round_of[0] = i
                if count:
                    count.offset = i * count.per_round
                for j in range(2):
                    late(FIRST + 2 * i + j, FIRST + j)
                    early(FIRST + 2 * i + j + 1, FIRST + j + 1)
            round_of[0] = 0
            if count:
                assert count.value - before_loop == count.per_round, count.value - before_loop
                count.offset, count.value = 0, before_loop + rounds * count.per_round
            for s in range(LAST + 1, BATCHES + 1):
                late(s, s)
                early(s + 1, s + 1)

        def by_heads(heads):
            return (lambda s, k: heads(s, k, range(SEAM, HEADS))), (lambda s, k: heads(s, k, range(SEAM)))

        def live(like, b):
            return 0 <= like + b < BATCHES

        round_of = [0]

        def pair(s, k, b):
            return (k + b) // 2 + 1 + round_of[0]

        def atleast(engine, semaphore, value, like):
            assert like or isinstance(round_of[0], int)
            if like > 0:
                engine.wait_ge(semaphore, value)

        def apart(engine, passed):
            if not isinstance(round_of[0], int):
                engine.sem_inc(passed, 1)

        free_from_start = {"pe": (Otr_ok, OT_ps), "dve": (x1_ok, slot_ok), "pool": (xbias_ok, pay_ok)}

        block = ctx.enter_context(nc.Block())

        @block.sync
        def _(sp):
            def x_rows(b):
                return x[bass.ds(b * T, T), :].rearrange("(t p) d -> p t d", p=128)

            sp.dma_start(xin[:, 0], x_rows(0)).then_inc(x_in[0], 16)
            sp.dma_start(C[:], cst).then_inc(cst_in, 16)
            sp.dma_start(W[:], wts).then_inc(wts_in, 16)
            sp.dma_start(bo_all[:], bo.partition_broadcast(128)).then_inc(bo_in, 16)
            sp.wait_ge(ones_set, 1)
            for p in range(2):
                sp.dma_start(QK[p][PART_ROWS:SCORE_ROWS, :, 1].bitcast(fp32), ones[:]).then_inc(ones_in, 16)

            def load_expert(e, j):
                sp.dma_start(w1s[:, j], w1[bass.ds(e * D, D), :]).then_inc(w_in[j], 16)
                sp.dma_start(w2s[:, j], w2[bass.ds(e * HIDDEN, HIDDEN), :].rearrange("(c p) d -> p c d", p=128)
                             ).then_inc(w_in[j], 16)
                sp.dma_start(b1s[:, j], b1[bass.ds(e * 128, 128), :]).then_inc(w_in[j], 16)
                sp.dma_start(b2s[:, j], b2[bass.ds(e, 1), :].rearrange("a d -> (a d)").partition_broadcast(128)
                             ).then_inc(w_in[j], 16)

            def moves(s, k):
                def move(half, b, kb):
                    p = kb % 2
                    if isinstance(b, int) and b < 2:
                        sp.wait_ge(zero_ok[p], half + 1)
                    atleast(sp, score_ok, (b - 2) * HEADS + (half + 1) * HALF, kb - 1)
                    sp.wait_ge(parts_ok, b + 1)
                    a, z = 64 * half, 64 * half + 64
                    for n, (lo, st) in enumerate([(0, 2), (0, 3), (1, 1)]):
                        sp.dma_start(QK[p][n * HD:(n + 1) * HD, half * HALF:(half + 1) * HALF].bitcast(fp32),
                                     parts[a:z, p, lo:lo + st + 1:st, :].bitcast(fp32)).then_inc(moved[half], 16)

                def move_max(half, b, kb):
                    p = kb % 2
                    sp.wait_ge(mT_ok, 2 * b + half + 1)
                    sp.dma_start(QK[p][PART_ROWS:SCORE_ROWS, half * HALF:(half + 1) * HALF, 0].bitcast(fp32),
                                 mT[:, half].bitcast(fp32)).then_inc(max_in[half], 16)

                return move, move_max

            def early(s, k):
                move, move_max = moves(s, k)
                if live(k, -1):
                    sp.wait_ge(xbias_ok, s)
                    sp.dma_start(xres[:], x_rows(s - 1)).then_inc(tail_dma, 16)
                if live(k, 1):
                    move(1, s + 1, k + 1)
                if live(k, 0):
                    move_max(1, s, k)

            def late(s, k):
                move, move_max = moves(s, k)
                if 1 <= k + 3 < BATCHES:
                    atleast(sp, xn1_ok, s + 2, k + 2)
                    sp.dma_start(xin[:, (k + 3) % 2], x_rows(s + 3)).then_inc(x_in[(k + 3) % 2], 16)
                if live(k, 2):
                    move(0, s + 2, k + 2)
                if live(k, 1):
                    move_max(0, s + 1, k + 1)
                if live(k, -1):
                    sp.wait_ge(x1_ok, s + 1)
                    sp.dma_start(out[bass.ds((s - 1) * T, T), :].rearrange("(t p) d -> p t d", p=128),
                                 x1[:]).then_inc(tail_dma, 16)
                if k == BATCHES - 2:
                    for e in range(2):
                        load_expert(e, e)

            steps(sp, late, early)
            for parity in range(2):
                sp.wait_ge(sent[parity], 16 + 16 * TILES * TOPK * BATCHES // 2)

            def load_rows(e, p):
                sp.dma_start(xe[:, p], rows[bass.ds(e * CAPACITY, CAPACITY), :].rearrange("(t p) r -> p t r", p=128)
                             ).then_inc(xe_in[p], 16)

            for e in range(4):
                load_rows(e, e)

            def refill(e):
                sp.wait_ge(ye_ps, e + 1)
                sp.wait_ge(yb_ok, e + 1)
                load_expert(e + 2, e % 2)

            for e in range(EXPERTS - 2):
                refill(e)
                if e < EXPERTS - 4:
                    sp.wait_ge(added, 16 * SLOT_TILES * (e + 1))
                    load_rows(e + 4, e)
            sp.wait_ge(added, 16 * SLOT_TILES * EXPERTS)

        @block.tensor
        def _(pe):
            mm, tr = nc.tensor.matmul, nc.tensor.transpose
            for free in free_from_start["pe"]:
                pe.sem_inc(free, 1)
            pe.wait_ge(wts_in, 16)
            pe.wait_ge(bv_ok, 1)
            mm(psC[:, 0:D], bv_rep[:], W[:, W_O:W_O + D], start=True, stop=True).then_inc(bias_ps, 1)
            pe.wait_ge(cst_in, 16)

            def heads(s, k, run):
                p = k % 2

                def x_transpose():
                    pe.wait_ge(xn1_ok, s + 3)
                    atleast(pe, mT_ok, 2 * s + 1, k + 1)
                    for t in range(TILES):
                        i = tr(psB[:, 128 * t:128 * t + 128], xn1[:, p, t], ident)
                    i.then_inc(xT_ps, 1)

                def project(ps, cols, wait_bank, done):
                    pe.wait_ge(xT_ok, s + 3)
                    wait_bank()
                    for n, c in enumerate(cols):
                        i = mm(ps[:, T * n:T * n + T], W[:, c:c + 128], xT[:, p], start=True, stop=True)
                    i.then_inc(done, 1)

                def project_v():
                    if live(k, 2):
                        pe.wait_ge(qk_ev, s + 3)
                    for t in range(TILES):
                        i = mm(psB[:, 128 * t:128 * t + 128], xT[:, 1 - p, 128 * t:128 * t + 128],
                               W[:, W_V:W_V + 128], start=True, stop=True)
                    i.then_inc(v_ps, 1)

                def max_transpose(half, b, kb, ps):
                    pe.wait_ge(mparts_ok, 2 * b + half + 1)
                    for t in range(TILES):
                        i = tr(ps[0:2 * HALF, 128 * t:128 * t + 128],
                               mparts[:, half, t].rearrange("p a h -> p (a h)").bitcast(fp32), ident)
                    i.then_inc(mT_ps, 1)

                def max_scores(h):
                    g = (s + 1) * HEADS + h
                    if h % HALF == 0:
                        pe.wait_ge(moved[h // HALF], 48 * (s + 2))
                    atleast(pe, max_ok, g - 1, (k + 1) * HEADS + h - 1)
                    for t in range(TILES):
                        i = mm(max_ps[h % 2][:, T * t:T * t + T], QK[1 - p][0:PART_ROWS, h, 0, 128 * t:128 * t + 128],
                               QK[1 - p][0:PART_ROWS, h, 1, :], start=True, stop=True)
                    i.then_inc(max_ps_ok, 1)

                def scores(h):
                    g = s * HEADS + h
                    if h % HALF == 0:
                        pe.wait_ge(max_in[h // HALF], 16 * (s + 1))
                    atleast(pe, prob_ok, g - 1, k * HEADS + h - 1)
                    for t in range(TILES):
                        i = mm(score_ps[h % 2][:, T * t:T * t + T], QK[p][0:SCORE_ROWS, h, 1, 128 * t:128 * t + 128],
                               QK[p][0:SCORE_ROWS, h, 0, :], start=True, stop=True)
                    i.then_inc(score_ok, 1)

                def values(b, kb, n):
                    grp, pos = n // 2, n % 2
                    pe.wait_ge(prob_ok, b * HEADS + 4 * n + 4)
                    if n == 0:
                        pe.wait_ge(v_ok, b + 1)
                        atleast(pe, O_ok, b, kb)
                    for t in range(TILES):
                        c = V_BASE[2 * t + pos] + 128 * grp
                        for j in range(4):
                            i = mm(pv_ps[32 * j:32 * j + 32, T * grp:T * grp + T],
                                   VA[:, kb % 2, c + 32 * j:c + 32 * j + 32],
                                   P[:, (4 * n + j) % 8, T * t:T * t + T],
                                   start=(pos == 0 and t == 0), stop=(pos == 1 and t == 1))
                    i.then_inc(pv_ok, 1)

                def o_transpose():
                    pe.wait_ge(O_ok, s)
                    pe.wait_ge(slot_ok, s)
                    for t in range(TILES):
                        for g in range(2):
                            i = tr(psC[:, 256 * t + 128 * g:256 * t + 128 * g + 128],
                                   O[:, g, 128 * t:128 * t + 128], ident)
                    i.then_inc(Otr_ok, 1)

                def on_transpose():
                    pe.wait_ge(On_ok, s)
                    for t in range(TILES):
                        i = tr(psC[:, 128 * t:128 * t + 128], On[:, t], ident)
                    i.then_inc(OT_ps, 1)

                def project_out():
                    pe.wait_ge(OT_ok, s)
                    for t in range(TILES):
                        i = mm(psC[:, 128 * t:128 * t + 128], OT[:, 128 * t:128 * t + 128], W[:, W_O:W_O + D],
                               start=True, stop=True)
                    i.then_inc(y_ok, 1)

                def xn2_transpose():
                    pe.wait_ge(xn2_ok, s - 1)
                    for t in range(TILES):
                        i = tr(psC[:, 128 * t:128 * t + 128], pay[:, p, 0, t, 0:D], ident)
                    i.then_inc(xn2T_ps, 1)

                def router():
                    pe.wait_ge(xn2T_ok, s - 1)
                    for t in range(TILES):
                        i = mm(logits(t), xn2T[:, 128 * t:128 * t + 128], W[:, W_R:W_R + EXPERTS], start=True, stop=True)
                    i.then_inc(logit_ok, 1)

                def positions():
                    pe.wait_ge(chosen_ok, s - 1)
                    mm(psC[:, POS:POS + TILES * EXPERTS], before[:], chosen[:].rearrange("p t e -> p (t e)"),
                       start=True, stop=False)
                    mm(psC[:, POS:POS + TILES * EXPERTS], every[:], seen[:, 0:TILES].rearrange("p t e -> p (t e)"),
                       start=False, stop=True).then_inc(pos_ok, 1)

                for h in run:
                    if live(k, 0):
                        scores(h)
                    if live(k, 1):
                        max_scores(h)
                    if k == 0 and h == 0:
                        pe.wait_ge(ones_in, 32)
                        pe.wait_ge(attn_bias_ok, 1)
                        pe.wait_ge(before_ok, 1)
                    if h == XT_H and live(k, 2):
                        x_transpose()
                    if h == 0 and live(k, -1):
                        values(s - 1, k - 1, 3)
                    if h == 1 and live(k, 0):
                        max_transpose(1, s, k, psA)
                    if h == 0 and live(k, -2):
                        xn2_transpose()
                    if h == 2 and live(k, -2):
                        router()
                    if h == XT_H + 2 and live(k, 2):
                        project(psB, (W_Q, W_K), lambda: None, qk_ps)
                    if h == XT_H + 3 and live(k, 2):
                        project(psA, (W_QS, W_KS), lambda: atleast(pe, mT_ok, 2 * s + 2, k + 1), qs_ps)
                    if h == 5 and live(k, -2):
                        positions()
                    if h == 5 and live(k, 0):
                        values(s, k, 0)
                    if h == 7 and live(k, -1):
                        o_transpose()
                    if h == 8 and live(k, 1):
                        project_v()
                    if h == 9 and live(k, -1):
                        on_transpose()
                    if h == 9 and live(k, 0):
                        values(s, k, 1)
                    if h == 11 and live(k, -1):
                        project_out()
                    if h == 11 and live(k, 1):
                        pe.wait_ge(v_ok, s + 2)
                        max_transpose(0, s + 1, k + 1, psB)
                    if h == 13 and live(k, 0):
                        values(s, k, 2)

            steps(pe, *by_heads(heads))

            pe.wait_ge(prob_ok, BATCHES * HEADS)
            pe.wait_ge(max_ok, BATCHES * HEADS)
            pe.wait_ge(mT_ok, 2 * BATCHES)
            pe.wait_ge(O_ok, BATCHES)

            def gather(e, r, q):
                pe.wait_ge(xe_in[q], 16 * (r + 1))
                pe.wait_ge(xeT_ok, e)
                for t in range(SLOT_TILES):
                    last = tr(bank[4][:, 128 * t:128 * t + 128], xe[:, q, t, 0:D], ident)
                last.then_inc(xeT_ps, 1)

            def expert(e, r, q, after):
                j = q % 2
                pe.wait_ge(w_in[j], 64 * (2 * r + q // 2 + 1))
                pe.wait_ge(xeT_ok, e + 1)
                for c in range(CHUNKS):
                    mm(bank[c][:, 0:CAPACITY], w1s[:, j, 128 * c:128 * c + 128], xeT[:, j], start=True, stop=True
                       ).then_inc(h_ps, 1)
                if after:
                    gather(e + 1, r + (q + 1) // 4, (q + 1) % 4)
                pe.wait_ge(yb_ok, e)
                for t in range(SLOT_TILES):
                    for c in range(CHUNKS):
                        if t == 0:
                            pe.wait_ge(hV_ok if c % 2 else hA_ok, 2 * e + c // 2 + 1)
                        last = mm(bank[5][:, 128 * t:128 * t + 128], hT[:, c, 128 * t:128 * t + 128],
                                  w2s[:, j, c], start=(c == 0), stop=(c == CHUNKS - 1))
                last.then_inc(ye_ps, 1)

            gather(0, 0, 0)
            for r in range(EXPERTS // 4):
                for q in range(4):
                    expert(4 * r + q, r, q, 4 * r + q < EXPERTS - 1)

        @block.scalar
        def _(act):
            fn = nc.scalar.activation
            act.wait_ge(wts_in, 16)
            act.wait_ge(va_set, 1)

            def heads(s, k, run):
                p = k % 2

                def probs(h):
                    g = s * HEADS + h
                    act.wait_ge(score_ok, g + 1)
                    if h % 4 == 0:
                        atleast(act, pv_ok, 4 * s + h // 4 - 1, 4 * k + h // 4 - 1)
                    fn(P[:, h % 8], score_ps[h % 2][:], ACT.Exp, scale=float(HD) ** -0.5).then_inc(prob_ok, 1)

                def copy_max(half, b, ps):
                    act.wait_ge(mT_ps, 2 * b + half + 1)
                    atleast(act, max_in[half], 16 * b, k + 1 - half)
                    fn(mT[:, half], ps[0:2 * HALF, 0:T], ACT.Copy).then_inc(mT_ok, 1)

                def copy_x():
                    act.wait_ge(xT_ps, s + 3)
                    atleast(act, v_ps, s + 1, k + 1)
                    fn(xT[:, p], psB[:, 0:T], ACT.Copy).then_inc(xT_ok, 1)

                def copy_v():
                    act.wait_ge(v_ps, s + 2)
                    atleast(act, pv_ok, 4 * s, k)
                    v = VA[:, 1 - p].rearrange("p (i r) -> p i r", r=V_STEP)[:, :, 0:256]
                    fn(v.rearrange("p i (g c) -> p i g c", c=32)[:, :, :, 0:HD],
                       psB[:, 0:2 * 128].rearrange("p (i g c) -> p i g c", i=4, c=HD), ACT.Copy).then_inc(v_ok, 1)

                def copy_o():
                    act.wait_ge(pv_ok, 4 * s)
                    act.wait_ge(Otr_ok, s)
                    fn(O[:].rearrange("p g t -> p (g t)"), pv_ps[:], ACT.Copy).then_inc(O_ok, 1)

                def copy_on():
                    act.wait_ge(OT_ps, s + 1)
                    fn(OT[:], psC[:, 0:T], ACT.Copy).then_inc(OT_ok, 1)

                def copy_xn2():
                    act.wait_ge(xn2T_ps, s - 1)
                    fn(xn2T[:], psC[:, 0:T], ACT.Copy).then_inc(xn2T_ok, 1)

                def second_rows():
                    act.wait_ge(xn2_ok, s - 1)
                    fn(pay[:, p, 1, :, 0:D], pay[:, p, 0, :, 0:D], ACT.Copy).then_inc(rows2_ok, 1)

                def exp_gap():
                    act.wait_ge(gap_ok, s - 1)
                    fn(e2[:], gap[:], ACT.Exp).then_inc(e2_ok, 1)

                for h in run:
                    if live(k, 0):
                        probs(h)
                    if h == 1 and live(k, -1):
                        copy_o()
                    if h == XT_H + 1 and live(k, 2):
                        copy_x()
                    if h == 2 and live(k, 0):
                        copy_max(1, s, psA)
                    if h == 1 and live(k, -2):
                        copy_xn2()
                    if h == 3 and live(k, -2):
                        second_rows()
                    if h == 5 and live(k, -2):
                        exp_gap()
                    if h == 10 and live(k, -1):
                        copy_on()
                    if h == 9 and live(k, 1):
                        copy_v()
                    if h == 12 and live(k, 1):
                        copy_max(0, s + 1, psB)

            steps(act, *by_heads(heads))

            def expert(e, j):
                act.wait_ge(xeT_ps, e + 1)
                fn(xeT[:, j], bank[4][:, 0:CAPACITY], ACT.Copy).then_inc(xeT_ok, 1)
                for c in (0, 2):
                    act.wait_ge(h_ps, 4 * e + c + 1)
                    act.wait_ge(ye_ps, e)
                    fn(hT[:, c], bank[c][:, 0:CAPACITY], ACT.Relu, bias=b1s[:, j, c:c + 1]).then_inc(hA_ok, 1)

            for e in range(EXPERTS):
                expert(e, e % 2)

        @block.vector
        def _(dve):
            V = nc.vector
            count = Count(DVE_LINKS)

            def link(ins, alone=False):
                ins.then_inc(dve_chain, 1)
                dve.wait_ge(dve_chain, count.next())
                if alone:
                    apart(dve, dve_passed)

            for free in free_from_start["dve"]:
                dve.sem_inc(free, 1)
            V.memset(ones[:], 1.0).then_inc(ones_set, 1)
            V.memset(QK[1][0:PART_ROWS, 0:HALF].bitcast(fp32), 0.0).then_inc(zero_ok[1], 1)
            link(V.memset(VA[:], 0.0))
            for p in range(2):
                for n in range(4):
                    c = V_BASE[n] + 9 * (n % 2) + HD
                    i = V.memset(VA[:, p, c:c + 32 * 7 + 1:32], 1.0)
            i.then_inc(va_set, 1)
            V.memset(seen[:], 0.0)

            def first_constants():
                dve.wait_ge(wts_in, 16)
                V.tensor_copy(bv_rep[:], W[:, W_BV:W_BV + 1].to_broadcast([128, 128])).then_inc(bv_ok, 1)
                V.memset(every[:], 1.0)
                V.tensor_copy(before[:], C[:, C_UP:C_UP + 128]).then_inc(before_ok, 1)

            def second_constants():
                dve.wait_ge(bias_ps, 1)
                dve.wait_ge(bo_in, 16)
                V.tensor_tensor(attn_bias[:], psC[:, 0:D], bo_all[:], ALU.add).then_inc(attn_bias_ok, 1)

            def heads(s, k, run):
                p = k % 2

                def reduce(h):
                    g = (s + 1) * HEADS + h
                    dve.wait_ge(max_ps_ok, g + 1)
                    V.tensor_reduce(negmax[:, h // HALF, :, h % HALF],
                                    max_ps[h % 2][:].rearrange("p (t k) -> p t k", t=TILES),
                                    axis=AX.X, op=ALU.max, negate=True).then_inc(max_ok, 1)

                def split_max(half):
                    dve.wait_ge(max_ok, (s + 1) * HEADS + (half + 1) * HALF)
                    atleast(dve, mT_ps, 2 * (s + 1) + half - 1, k + 1)
                    link(V.tensor_copy(mparts[:, half, :, 0], negmax[:, half]))
                    V.tensor_tensor(mparts[:, half, :, 1], negmax[:, half], mparts[:, half, :, 0].bitcast(fp32),
                                    ALU.subtract).then_inc(mparts_ok, 1)

                def norm1_stats():
                    b = (k + 3) % 2
                    dve.wait_ge(x_in[b], 16 * pair(s, k, 3))
                    atleast(dve, xn1_ok, s + 2, k + 2)
                    for t in range(TILES):
                        i = V.bn_stats(stats1[:, b, t], xin[:, b, t])
                    link(i, True)
                    for t in range(TILES):
                        i = V.bn_aggr(mv1[:, b, t], stats1[:, b, t])
                    i.then_inc(stats1_ok, 1)

                def norm1():
                    b = (k + 3) % 2
                    dve.wait_ge(rstd1_ok, s + 4)
                    atleast(dve, xT_ps, s + 2, k + 2)
                    for t in range(TILES):
                        i = V.tensor_scalar(xn1[:, b, t], xin[:, b, t], mv1[:, b, t, 0:1], rstd1[:, b, t:t + 1],
                                            ALU.subtract, ALU.mult)
                    i.then_inc(xn1_ok, 1)

                def norm2():
                    dve.wait_ge(rstd2_ok, s)
                    for t in range(TILES):
                        i = V.tensor_scalar(pay[:, 1 - p, 0, t, 0:D], x1[:, t], mv2[:, t, 0:1], rstd2[:, t:t + 1],
                                            ALU.subtract, ALU.mult)
                    i.then_inc(xn2_ok, 1)

                def rotate(ps, ready, first, table, into, done):
                    dve.wait_ge(ready, s + 3)
                    atleast(dve, rope_ok, s + 2, k + 2)
                    for n in range(2):
                        i = V.scalar_tensor_tensor(
                            out=into[:, n], in0=ps[:, T * n:T * n + T],
                            scalar=W[:, W_BIAS + first + n:W_BIAS + first + n + 1], in1=C[:, table:table + T],
                            op0=ALU.add, op1=ALU.mult)
                    i.then_inc(done, 1)

                def normalise():
                    dve.wait_ge(Otr_ok, s + 1)
                    o = psC[:].rearrange("p (a c) -> p a c", c=32)[:, :, 0:18].rearrange("p a (b r) -> p a b r", r=9)
                    link(V.reciprocal(rsum[:].unsqueeze(3), o[:, :, :, HD:HD + 1]))
                    dve.wait_ge(OT_ps, s)
                    V.tensor_tensor(On[:].rearrange("p t (a b d) -> p (t a) b d", b=2, d=HD), o[:, :, :, 0:HD],
                                    rsum[:].unsqueeze(3).to_broadcast([128, TILES * 8, 2, HD]), ALU.mult
                                    ).then_inc(On_ok, 1)

                def residual():
                    dve.wait_ge(y_ok, s)
                    dve.wait_ge(xbias_ok, s + 1)
                    dve.wait_ge(tail_dma, 16 * (2 * s - 1))
                    dve.wait_ge(pay_ok, s)
                    link(V.tensor_tensor(x1[:], psC[:, 0:T].rearrange("p (t d) -> p t d", t=TILES), xbias[:], ALU.add))
                    for t in range(TILES):
                        i = V.bn_stats(stats2[:, t], x1[:, t])
                    link(i, True)
                    for t in range(TILES):
                        i = V.bn_aggr(mv2[:, t], stats2[:, t])
                    i.then_inc(x1_ok, 1)

                def choose():
                    dve.wait_ge(logit_ok, s - 1)
                    apart(dve, dve_passed)
                    for t in range(TILES):
                        i = V.max(best[:, t], logits(t))
                    link(i, True)
                    for t in range(TILES):
                        i = V.max_index(besti[:, t], best[:, t], logits(t))
                    V.tensor_tensor(gap[:], best[:, :, 1], best[:, :, 0], ALU.subtract).then_inc(gap_ok, 1)
                    dve.wait_ge(gap_ok, s - 1)
                    link(V.tensor_copy(choice[:], besti[:, :, 0:TOPK]))
                    link(V.tensor_tensor(
                        onehot[:], choice[:].unsqueeze(3).to_broadcast([128, TILES, TOPK, EXPERTS]),
                        C[:, C_IOTA:C_IOTA + TILES * TOPK * EXPERTS].rearrange("p (t k e) -> p t k e", t=TILES, k=TOPK),
                        ALU.is_equal))
                    link(V.tensor_tensor(chosen[:], onehot[:, :, 0], onehot[:, :, 1], ALU.add))
                    link(V.tensor_tensor(seen[:, 1], seen[:, 0], chosen[:, 0], ALU.add))
                    V.tensor_tensor(seen[:, 2], seen[:, 1], chosen[:, 1], ALU.add).then_inc(chosen_ok, 1)

                def place():
                    dve.wait_ge(pos_ok, s - 1)
                    dve.wait_ge(e2_ok, s - 1)
                    dve.wait_ge(pay_ok, s)
                    for t in range(TILES):
                        i = V.tensor_tensor(
                            hit[:, t], onehot[:, t],
                            psC[:, POS + EXPERTS * t:POS + EXPERTS * t + EXPERTS].unsqueeze(1).to_broadcast(
                                [128, TOPK, EXPERTS]), ALU.mult)
                    link(i)
                    V.tensor_reduce(slot[:], hit[:], axis=AX.X, op=ALU.add)
                    V.tensor_copy(seen[:, 0], seen[:, 2])
                    link(V.tensor_scalar(den[:], e2[:], 1.0, None, ALU.add))
                    V.tensor_scalar(over[:], slot[:], float(CAPACITY), float(NOWHERE), ALU.is_ge, ALU.mult)
                    V.scalar_tensor_tensor(out=base[:], in0=choice[:], scalar=float(CAPACITY), in1=slot[:],
                                           op0=ALU.mult, op1=ALU.add)
                    link(V.reciprocal(pay[:, p, 0, :, D:D + 1], den[:].unsqueeze(2)))
                    V.tensor_tensor(dest[:, p], base[:], over[:], ALU.add)
                    V.tensor_tensor(pay[:, p, 1, :, D], pay[:, p, 0, :, D], e2[:], ALU.mult).then_inc(slot_ok, 1)

                for h in run:
                    if live(k, 1):
                        reduce(h)
                        if h % HALF == HALF - 1:
                            split_max(h // HALF)
                    if h == 2 and live(k, -2):
                        choose()
                    if h == XT_H + 2 and live(k, 2):
                        rotate(psB, qk_ps, 0, C_COS, rot1, qk_ev)
                    if h == XT_H + 3 and live(k, 2):
                        rotate(psA, qs_ps, 2, C_SIN, rot2, qs_ev)
                    if h == 6 and live(k, -2):
                        place()
                    if h == 8 and live(k, -1):
                        normalise()
                    if h == 9 and live(k, 3):
                        norm1_stats()
                        if k == -3:
                            first_constants()
                        if k == -2:
                            second_constants()
                            V.memset(QK[1][0:PART_ROWS, HALF:HEADS].bitcast(fp32), 0.0).then_inc(zero_ok[1], 1)
                    if h == 11 and live(k, 3):
                        norm1()
                    if h == 12 and live(k, -1):
                        residual()
                    if h == 14 and live(k, -1):
                        norm2()

            steps(dve, *by_heads(heads), count)

            def expert(e, j):
                for c in (1, 3):
                    dve.wait_ge(h_ps, 4 * e + c + 1)
                    dve.wait_ge(ye_ps, e)
                    V.tensor_scalar(hT[:, c], bank[c][:, 0:CAPACITY], b1s[:, j, c:c + 1], 0.0, ALU.add, ALU.max
                                    ).then_inc(hV_ok, 1)
                dve.wait_ge(ye_ps, e + 1)
                dve.wait_ge(yg_ok, e)
                V.tensor_tensor(yb[:], bank[5][:, 0:CAPACITY].rearrange("p (t d) -> p t d", d=D),
                                b2s[:, j].unsqueeze(1).to_broadcast([128, SLOT_TILES, D]), ALU.add
                                ).then_inc(yb_ok, 1)

            for e in range(EXPERTS):
                expert(e, e % 2)

        @block.gpsimd
        def _(pool):
            G = nc.gpsimd
            count = Count(POOL_LINKS)

            def link(ins):
                ins.then_inc(pool_chain, 1)
                pool.wait_ge(pool_chain, count.next())
                apart(pool, pool_passed)

            for free in free_from_start["pool"]:
                pool.sem_inc(free, 1)
            G.memset(QK[0][0:PART_ROWS, 0:HALF].bitcast(fp32), 0.0).then_inc(zero_ok[0], 1)
            link(G.memset(minus_half[:], -0.5))

            def inverse_deviation(mv, rstd, done):
                link(G.tensor_scalar(rstd, mv[:, :, 1], 1.0, EPS, ALU.mult, ALU.add))
                G.tensor_tensor(rstd, rstd, minus_half[:], ALU.pow).then_inc(done, 1)

            def norm1(s, k):
                b = (k + 3) % 2
                pool.wait_ge(stats1_ok, s + 4)
                apart(pool, pool_passed)
                inverse_deviation(mv1[:, b], rstd1[:, b], rstd1_ok)

            def split_rope(s, k):
                p = k % 2
                pool.wait_ge(qk_ev, s + 3)
                pool.wait_ge(qs_ev, s + 3)
                G.tensor_tensor(rope[:], rot1[:], rot2[:], ALU.add).then_inc(rope_ok, 1)
                for half in range(2):
                    atleast(pool, moved[half], 48 * (s + 1), k + 1)
                pool.wait_ge(rope_ok, s + 3)
                apart(pool, pool_passed)
                G.tensor_scalar(parts[:, p, 0:4:2], rope[:], 1.0, 0.0, ALU.mult, ALU.add).then_inc(hi_ok, 1)
                pool.wait_ge(hi_ok, s + 3)
                G.tensor_tensor(parts[:, p, 1:4:2], rope[:], parts[:, p, 0:4:2].bitcast(fp32), ALU.subtract
                                ).then_inc(parts_ok, 1)

            def add_residual(s, k):
                pool.wait_ge(tail_dma, 16 * (2 * s - 1))
                pool.wait_ge(x1_ok, s)
                if k == 1:
                    pool.wait_ge(attn_bias_ok, 1)
                G.tensor_tensor(xbias[:], xres[:], attn_bias[:].unsqueeze(1).to_broadcast([128, TILES, D]), ALU.add
                                ).then_inc(xbias_ok, 1)

            def norm2(s, k):
                p = (k - 1) % 2
                pool.wait_ge(x1_ok, s + 1)
                pool.wait_ge(sent[p], 16 + 16 * TILES * TOPK * pair(s, k, -3))
                if k == 1:
                    pool.wait_ge(sent[1 - p], 16)
                apart(pool, pool_passed)
                inverse_deviation(mv2[:], rstd2[:], rstd2_ok)
                link(G.tensor_copy(pay[:, p, :, :, D + 1].bitcast(i32), tok[:].unsqueeze(1).to_broadcast(
                    [128, TOPK, TILES])))
                G.tensor_scalar(tok[:], tok[:], 1.0, float(T), ALU.mult, ALU.add).then_inc(pay_ok, 1)

            def dispatch(s, k, t):
                p = k % 2
                if t == 0:
                    pool.wait_ge(slot_ok, s)
                    pool.wait_ge(rows2_ok, s - 1)
                    apart(pool, pool_passed)
                for c in range(TOPK):
                    G.indirect_dma_start(
                        out=rows, out_offset=bass.IndirectOffsetOnAxis(ap=dest[:, p, t, c:c + 1], axis=0),
                        in_=pay[:, p, c, t], in_offset=None, bounds_check=SLOTS - 1, oob_is_err=False,
                    ).then_inc(sent[p], 16)

            def early(s, k):
                if live(k, -1):
                    add_residual(s, k)
                if live(k, 2):
                    split_rope(s, k)
                if live(k, -2):
                    dispatch(s, k, 0)
                    dispatch(s, k, 1)

            def late(s, k):
                if live(k, 3):
                    norm1(s, k)
                if live(k, -1):
                    norm2(s, k)
                if k == -3:
                    G.memset(QK[0][0:PART_ROWS, HALF:HEADS].bitcast(fp32), 0.0).then_inc(zero_ok[0], 1)
                    link(G.memset(blank[:], 0.0))
                    G.memset(blank[:, :, D + 1:D + 2].bitcast(i32), NOWHERE).then_inc(blank_set, 1)
                    pool.wait_ge(blank_set, 1)
                    for n in range(2):
                        G.dma_start(rows.rearrange("(n p r) d -> n p r d", n=2, p=128)[n],
                                    blank[:, 0:SLOTS // 256]).then_inc(sent[n], 16)
                    pool.wait_ge(cst_in, 16)
                    link(G.tensor_copy(tok[:], C[:, C_TOK:C_TOK + TILES]))

            steps(pool, late, early, count)
            pool.wait_ge(tail_dma, 16 * 2 * BATCHES)

            def expert(e, q):
                pool.wait_ge(yb_ok, e + 1)
                G.tensor_tensor(yg[:, q % 2], yb[:], xe[:, q, :, D:D + 1].to_broadcast([128, SLOT_TILES, D]), ALU.mult
                                ).then_inc(yg_ok, 1)
                pool.wait_ge(yg_ok, e + 1)
                atleast(pool, added, 16 * SLOT_TILES * e, e)
                for t in range(SLOT_TILES):
                    G.indirect_dma_start(
                        out=out, out_offset=bass.IndirectOffsetOnAxis(ap=xe[:, q, t, D + 1:D + 2].bitcast(i32), axis=0),
                        in_=yg[:, q % 2, t], in_offset=None, bounds_check=TOKENS - 1, oob_is_err=False,
                        compute_op=ALU.add).then_inc(added, 16)

            for e in range(EXPERTS):
                expert(e, e % 4)


def kernel(**inputs):
    import numpy as np
    import concourse.bacc as bacc
    from concourse.bass_utils import run_bass_kernel_spmd

    f = {n: np.asarray(a) for n, a in inputs.items()}
    qk = np.arange(D).reshape(2, HALF, HD).transpose(0, 2, 1).ravel()
    swapped = np.arange(D).reshape(2, HALF, HD)[:, :, np.arange(HD) ^ 1].transpose(0, 2, 1).ravel()
    vcols = np.arange(D).reshape(2, 2, 4, HD).transpose(1, 0, 2, 3).ravel()
    orows = np.arange(D).reshape(2, 2, 4, HD).transpose(0, 2, 1, 3).ravel()
    p = "L0_attn_"
    wq, wk, wv, wo = (f[p + n] for n in ("Wq", "Wk", "Wv", "Wo"))
    bq, bk, bv = (f[p + n] for n in ("bq", "bk", "bv"))
    wts = np.concatenate([
        wq[qk].T, wk[qk].T, wq[swapped].T, wk[swapped].T, wv[vcols].T, wo[:, orows].T, f["L0_ffn_w_router"],
        bq[qk][:, None], bk[qk][:, None], bq[swapped][:, None], bk[swapped][:, None], bv[orows][:, None]], axis=1)

    freq = (np.float32(1) / np.float32(10000) ** (np.arange(0, HD, 2, dtype=np.float32) / np.float32(HD)))
    angle = np.repeat(np.arange(T, dtype=np.float32)[:, None] * freq[None, :], 2, axis=-1).astype(np.float32)
    cos, sin = np.cos(angle), np.sin(angle) * np.where(np.arange(HD) % 2 == 0, -1, 1).astype(np.float32)
    row_feature = np.tile(np.repeat(np.arange(HD), HALF), 2)
    part = np.arange(128)
    cst = np.concatenate([
        np.eye(128), cos.T[row_feature], sin.T[row_feature], part[:, None] < part[None, :],
        np.tile(np.arange(EXPERTS), (128, TILES * TOPK)), part[:, None] + 128 * np.arange(TILES)[None, :],
    ], axis=1).astype(np.float32)

    arrays = {
        "x": f[p + "x"].reshape(TOKENS, D), "wts": wts, "cst": cst, "bo": f[p + "bo"],
        "w1": f["L0_ffn_w1"].reshape(EXPERTS * D, HIDDEN),
        "b1": f["L0_ffn_b1"].reshape(EXPERTS, CHUNKS, 128).transpose(0, 2, 1).reshape(EXPERTS * 128, CHUNKS),
        "w2": f["L0_ffn_w2"].reshape(EXPERTS * HIDDEN, D), "b2": f["L0_ffn_b2"],
    }
    arrays = {n: np.ascontiguousarray(a) for n, a in arrays.items()}
    nc = bacc.Bacc("TRN2", target_bir_lowering=False, num_devices=1)
    args = {n: nc.dram_tensor(n, a.shape, mybir.dt.from_np(a.dtype), kind="ExternalInput").ap()
            for n, a in arrays.items()}
    out = nc.dram_tensor("out", (TOKENS, D), mybir.dt.float32, kind="ExternalOutput").ap()
    rows = nc.dram_tensor("rows", (SLOTS, ROW), mybir.dt.float32, kind="Internal").ap()
    build(nc, **args, out=out, rows=rows)
    r = run_bass_kernel_spmd(nc, [arrays], core_ids=[0])
    return r.results[0]["out"].reshape(BATCHES, T, D)
```

```python
import concourse.bass as bass
from concourse import mybir
from contextlib import ExitStack

BATCHES, T, D = 8, 256, 128
HEADS, HD = 16, 8
TILES = T // 128
TOKENS = BATCHES * T
EXPERTS, HIDDEN, TOPK = 8, 512, 2
CAPACITY = int(1.5 * 4 * 256 * TOPK / EXPERTS)
SLOT_TILES = CAPACITY // 128
CHUNKS = HIDDEN // 128
SLOTS = EXPERTS * CAPACITY
OUT_ROWS = TOKENS + CAPACITY
ROW = D + 2
NOWHERE = 1 << 20
EPS = 1e-5
HALF = HEADS // 2

PART_ROWS = 96
SCORE_ROWS = PART_ROWS + 2

W_Q, W_K, W_QS, W_KS, W_V, W_O, W_R = 0, 128, 256, 384, 512, 640, 768
W_BIAS = W_R + EXPERTS
W_BV = W_BIAS + 4
W_COLS = W_BV + 1
C_ID, C_COS, C_SIN, C_UP, C_IOTA = 0, 128, 128 + T, 128 + 2 * T, 256 + 2 * T
C_TOK = C_IOTA + TILES * TOPK * EXPERTS
C_SPARE = C_TOK + TILES
C_COLS = C_SPARE + SLOT_TILES

V_STEP = 265
V_BASE = [V_STEP * i - 9 * (i % 2) for i in range(4)]
V_COLS = 4 * V_STEP

FIRST, LAST = 1, 4
LOGITS, POS = 256, 320
SEAM = 8
DVE_LINKS, POOL_LINKS = 12, 10


class Count:

    def __init__(self, per_round):
        self.value, self.offset, self.per_round = 0, 0, per_round

    def in_loop(self):
        return not isinstance(self.offset, int)

    def next(self):
        self.value += 1
        return self.value + self.offset


def build(nc, x, wts, cst, bo, w1, b1, w2, b2, out, rows):
    fp32, fp32r, bf16 = mybir.dt.float32, mybir.dt.float32r, mybir.dt.bfloat16
    i32, u32 = mybir.dt.int32, mybir.dt.uint32
    ALU, ACT, AX = mybir.AluOpType, mybir.ActivationFunctionType, mybir.AxisListType
    ctx = ExitStack()
    with ctx:
        def sb(name, shape, dt=fp32):
            return ctx.enter_context(nc.sbuf_tensor(name, shape, dt))

        def sem(name):
            return ctx.enter_context(nc.semaphore(name))

        bank = [ctx.enter_context(nc.psum_tensor(f"bank{i}", [128, 512], fp32)) for i in range(8)]
        score_ps, max_ps, pv_ps = bank[0:2], [bank[2], bank[3], bank[5]], bank[4]
        psB, psC = bank[6], bank[7]

        W = sb("W", [128, W_COLS])
        C = sb("C", [128, C_COLS])
        bo_all = sb("bo_all", [128, D])
        ones = sb("ones", [2 * HEADS, T])
        bv_rep = sb("bv_rep", [128, 128])
        attn_bias = sb("attn_bias", [128, D])
        before = sb("before", [128, 128], bf16)
        every = sb("every", [128, 128], bf16)
        minus_half = sb("minus_half", [128, TILES])
        blank = sb("blank", [128, SLOT_TILES, ROW])
        ident = C[:, C_ID:C_ID + 128]

        def logits(t):
            return psC[:, LOGITS + EXPERTS * t:LOGITS + EXPERTS * t + EXPERTS]


        xin = sb("xin", [128, 2, TILES, D])
        stats1 = sb("stats1", [128, 2, TILES, 6])
        mv1 = sb("mv1", [128, 2, TILES, 2])
        rstd1 = sb("rstd1", [128, 2, TILES])
        shift1 = sb("shift1", [128, 2, TILES])
        xn1 = sb("xn1", [128, 2, TILES, D])
        xT = sb("xT", [128, 2, T])
        rot1 = sb("rot1", [128, 2, T])
        rot2 = sb("rot2", [128, 2, T])
        rope = sb("rope", [128, 2, T])
        parts = sb("parts", [128, 2, 4, T], fp32r)
        QK = [sb(f"QK{p}", [SCORE_ROWS, HEADS, 2, T], fp32r) for p in range(2)]
        VA = sb("VA", [128, 2, V_COLS])
        negmax = sb("negmax", [128, 2, TILES, HALF])
        mparts = sb("mparts", [128, 2, TILES, 2, HALF], fp32r)
        mT = sb("mT", [2 * HALF, 2, T], fp32r)
        P = sb("P", [128, 8, 2 * T])
        O = sb("O", [128, 2, T])
        rsum = sb("rsum", [128, TILES * 8, 2])
        On = sb("On", [128, TILES, D])
        OT = sb("OT", [128, T])
        xres = sb("xres", [128, TILES, D])
        xbias = sb("xbias", [128, TILES, D])
        x1 = sb("x1", [128, TILES, D])
        stats2 = sb("stats2", [128, TILES, 6])
        mv2 = sb("mv2", [128, TILES, 2])
        rstd2 = sb("rstd2", [128, TILES])
        shift2 = sb("shift2", [128, TILES])
        pay = sb("pay", [128, 2, TOPK, TILES, ROW])
        xn2T = sb("xn2T", [128, T])
        best = sb("best", [128, TILES, 8])
        besti = sb("besti", [128, TILES, 8], u32)
        gap = sb("gap", [128, TILES])
        e2 = sb("e2", [128, TILES])
        den = sb("den", [128, TILES])
        onehot = sb("onehot", [128, TILES, TOPK, EXPERTS], bf16)
        chosen = sb("chosen", [128, EXPERTS])
        seen = sb("seen", [128, EXPERTS], bf16)
        hit = sb("hit", [128, TILES, TOPK, EXPERTS])
        slot = sb("slot", [128, TILES, TOPK])
        over = sb("over", [128, TILES, TOPK])
        base = sb("base", [128, TILES, TOPK])
        dest = sb("dest", [128, 2, TILES, TOPK], i32)
        tok = sb("tok", [128, TILES])
        warm = sb("warm", [128, 1])

        w1s = sb("w1s", [128, 2, HIDDEN])
        w2s = sb("w2s", [128, 2, CHUNKS, D])
        xe = sb("xe", [128, 2, SLOT_TILES, ROW])
        gate = sb("gate", [128, 2, SLOT_TILES])
        token = sb("token", [128, 2, SLOT_TILES], i32)
        b1s = sb("b1s", [128, 2, CHUNKS])
        b2s = sb("b2s", [128, 2, D])
        xeT = sb("xeT", [128, 2, 2, CAPACITY], fp32r)
        w1p = sb("w1p", [128, 2, 2, HIDDEN], fp32r)
        hT = sb("hT", [128, CHUNKS, CAPACITY])
        yb = sb("yb", [128, SLOT_TILES, D])
        yg = sb("yg", [128, 2, SLOT_TILES, D])

        wts_in, cst_in, bo_in = sem("wts_in"), sem("cst_in"), sem("bo_in")
        bias_ps, attn_bias_ok, bv_ok, before_ok, va_set, ones_set, ones_in = (
            sem(n) for n in ("bias_ps", "attn_bias_ok", "bv_ok", "before_ok", "va_set", "ones_set", "ones_in"))
        blank_set, spare_ok = sem("blank_set"), sem("spare_ok")
        zero_ok = [[sem(f"zero_ok{p}{h}") for h in range(2)] for p in range(2)]
        x_in = [sem("x_in0"), sem("x_in1")]
        stats1_ok, xn1_ok = sem("stats1_ok"), sem("xn1_ok")
        xT_ps, xT_ok, qk_ps, qs_ps, qk_ev, qs_ev = (
            sem(n) for n in ("xT_ps", "xT_ok", "qk_ps", "qs_ps", "qk_ev", "qs_ev"))
        v_ps, v_ok, rope_ok, hi_ok, parts_ok = (sem(n) for n in ("v_ps", "v_ok", "rope_ok", "hi_ok", "parts_ok"))
        moved = [sem("moved0"), sem("moved1")]
        max_ps_ok, max_ok, mparts_ok, mT_ps, mT_ok = (
            sem(n) for n in ("max_ps_ok", "max_ok", "mparts_ok", "mT_ps", "mT_ok"))
        max_in = [sem("max_in0"), sem("max_in1")]
        score_ok, prob_ok, pv_ok, O_ok = sem("score_ok"), sem("prob_ok"), sem("pv_ok"), sem("O_ok")
        Otr_ok, On_ok, OT_ps, OT_ok, y_ok = (sem(n) for n in ("Otr_ok", "On_ok", "OT_ps", "OT_ok", "y_ok"))
        xbias_ok, x1_ok, stats2_ok, rstd1_ok, rstd2_ok, shift1_ok, shift2_ok, xn2_ok = (
            sem(n) for n in ("xbias_ok", "x1_ok", "stats2_ok", "rstd1_ok", "rstd2_ok", "shift1_ok", "shift2_ok",
                             "xn2_ok"))
        tail_dma = sem("tail_dma")
        xn2T_ps, xn2T_ok, logit_ok, gap_ok, e2_ok, chosen_ok = (
            sem(n) for n in ("xn2T_ps", "xn2T_ok", "logit_ok", "gap_ok", "e2_ok", "chosen_ok"))
        pos_ok, hit_ok, slot_ok, pay_ok, rows2_ok = (
            sem(n) for n in ("pos_ok", "hit_ok", "slot_ok", "pay_ok", "rows2_ok"))
        sent = [sem("sent0"), sem("sent1")]
        w_in, xe_in = [sem(f"w_in{n}") for n in range(2)], [sem(f"xe_in{n}") for n in range(2)]
        w1_in = [sem("w1_in0"), sem("w1_in1")]
        token_ok, xelo_ok, w1hi_ok, w1p_ok = (sem(n) for n in ("token_ok", "xelo_ok", "w1hi_ok", "w1p_ok"))
        xeT_ps, xeT_ok, h_ps, hA_ok, hV_ok, ye_ps, yb_ok, yg_ok, added = (
            sem(n) for n in ("xeT_ps", "xeT_ok", "h_ps", "hA_ok", "hV_ok", "ye_ps", "yb_ok", "yg_ok", "added"))
        dve_chain, pool_chain = sem("dve_chain"), sem("pool_chain")
        dve_passed, pool_passed = sem("dve_passed"), sem("pool_passed")

        def steps(engine, late, early, count=None):
            rounds = (LAST - FIRST + 1) // 2
            for s in range(-4, FIRST):
                late(s, s)
                early(s + 1, s + 1)
            before_loop = count.value if count else 0
            with engine.Fori(0, rounds) as i:
                round_of[0] = i
                if count:
                    count.offset = i * count.per_round
                for j in range(2):
                    late(FIRST + 2 * i + j, FIRST + j)
                    early(FIRST + 2 * i + j + 1, FIRST + j + 1)
            round_of[0] = 0
            if count:
                assert count.value - before_loop == count.per_round, count.value - before_loop
                count.offset, count.value = 0, before_loop + rounds * count.per_round
            for s in range(LAST + 1, BATCHES + 1):
                late(s, s)
                early(s + 1, s + 1)

        def by_heads(heads):
            return (lambda s, k: heads(s, k, range(SEAM, HEADS))), (lambda s, k: heads(s, k, range(SEAM)))

        def live(like, b):
            return 0 <= like + b < BATCHES

        def max_bank(p, h):
            return max_ps[(h + 1 - p) % 3]

        def out_bank(like):
            return bank[5] if like == BATCHES else psC

        def at(like, head, last):
            return last if like == BATCHES else head

        round_of = [0]

        def pair(s, k, b):
            return (k + b) // 2 + 1 + round_of[0]

        def atleast(engine, semaphore, value, like):
            assert like or isinstance(round_of[0], int)
            if like > 0:
                engine.wait_ge(semaphore, value)

        def apart(engine, passed):
            if not isinstance(round_of[0], int):
                engine.sem_inc(passed, 1)

        def experts(engine, run):
            run(0, 0, 0)
            with engine.Fori(0, (EXPERTS - 2) // 2) as i:
                round_of[0] = i
                run(2 * i + 1, 1, i)
                run(2 * i + 2, 0, i + 1)
            round_of[0] = 0
            run(EXPERTS - 1, 1, EXPERTS // 2 - 1)

        def split_rope(engine, ops, passed, s, k):
            p = k % 2
            engine.wait_ge(qk_ev, s + 3)
            engine.wait_ge(qs_ev, s + 3)
            ops.tensor_tensor(rope[:], rot1[:], rot2[:], ALU.add).then_inc(rope_ok, 1)
            for half in range(2):
                atleast(engine, moved[half], 48 * (s + 1), k + 1)
            engine.wait_ge(rope_ok, s + 3)
            apart(engine, passed)
            ops.tensor_scalar(parts[:, p, 0:4:2], rope[:], 1.0, 0.0, ALU.mult, ALU.add).then_inc(hi_ok, 1)
            engine.wait_ge(hi_ok, s + 3)
            ops.tensor_tensor(parts[:, p, 1:4:2], rope[:], parts[:, p, 0:4:2].bitcast(fp32), ALU.subtract
                              ).then_inc(parts_ok, 1)

        def is_number(e, value):
            return isinstance(e, int) and e == value

        free_from_start = {"pe": (Otr_ok, OT_ps), "act": (x1_ok, xn2_ok), "dve": (hit_ok,), "pool": (xbias_ok, pay_ok)}

        block = ctx.enter_context(nc.Block())

        @block.sync
        def _(sp):
            def x_rows(b):
                return x[bass.ds(b * T, T), :].rearrange("(t p) d -> p t d", p=128)

            sp.dma_start(xin[:, 0], x_rows(0)).then_inc(x_in[0], 16)
            sp.dma_start(C[:], cst).then_inc(cst_in, 16)
            sp.dma_start(W[:], wts).then_inc(wts_in, 16)
            sp.dma_start(bo_all[:], bo.partition_broadcast(128)).then_inc(bo_in, 16)
            sp.wait_ge(ones_set, 1)
            for p in range(2):
                sp.dma_start(QK[p][PART_ROWS:SCORE_ROWS, :, 1].bitcast(fp32), ones[:]).then_inc(ones_in, 16)

            def load_w1(e, j):
                sp.dma_start(w1s[:, j], w1[bass.ds(e * D, D), :]).then_inc(w1_in[j], 16)

            def load_expert(e, j):
                sp.dma_start(w2s[:, j], w2[bass.ds(e * HIDDEN, HIDDEN), :].rearrange("(c p) d -> p c d", p=128)
                             ).then_inc(w_in[j], 16)
                sp.dma_start(b1s[:, j], b1[bass.ds(e * 128, 128), :]).then_inc(w_in[j], 16)
                sp.dma_start(b2s[:, j], b2[bass.ds(e, 1), :].rearrange("a d -> (a d)").partition_broadcast(128)
                             ).then_inc(w_in[j], 16)

            def moves(s, k):
                def move(half, b, kb):
                    p = kb % 2
                    if isinstance(b, int) and b < 2:
                        sp.wait_ge(zero_ok[p][half], 1)
                    atleast(sp, score_ok, (b - 2) * HEADS + (half + 1) * HALF, kb - 1)
                    sp.wait_ge(parts_ok, b + 1)
                    a, z = 64 * half, 64 * half + 64
                    for n, (lo, st) in enumerate([(0, 2), (0, 3), (1, 1)]):
                        sp.dma_start(QK[p][n * HD:(n + 1) * HD, half * HALF:(half + 1) * HALF].bitcast(fp32),
                                     parts[a:z, p, lo:lo + st + 1:st, :].bitcast(fp32)).then_inc(moved[half], 16)

                def move_max(half, b, kb):
                    p = kb % 2
                    sp.wait_ge(mT_ok, 2 * b + half + 1)
                    sp.dma_start(QK[p][PART_ROWS:SCORE_ROWS, half * HALF:(half + 1) * HALF, 0].bitcast(fp32),
                                 mT[:, half].bitcast(fp32)).then_inc(max_in[half], 16)

                return move, move_max

            def early(s, k):
                move, move_max = moves(s, k)
                if live(k, -1):
                    sp.wait_ge(xbias_ok, s)
                    sp.dma_start(xres[:], x_rows(s - 1)).then_inc(tail_dma, 16)
                if live(k, 1):
                    move(1, s + 1, k + 1)
                if live(k, 0):
                    move_max(1, s, k)

            def late(s, k):
                move, move_max = moves(s, k)
                if 1 <= k + 3 < BATCHES:
                    atleast(sp, xn1_ok, s + 2, k + 2)
                    sp.dma_start(xin[:, (k + 3) % 2], x_rows(s + 3)).then_inc(x_in[(k + 3) % 2], 16)
                if live(k, 2):
                    move(0, s + 2, k + 2)
                if live(k, 1):
                    move_max(0, s + 1, k + 1)
                if live(k, -1):
                    sp.wait_ge(x1_ok, s + 1)
                    sp.dma_start(out[bass.ds((s - 1) * T, T), :].rearrange("(t p) d -> p t d", p=128),
                                 x1[:]).then_inc(tail_dma, 16)
                if k == BATCHES - 2:
                    for e in range(2):
                        load_w1(e, e)
                        load_expert(e, e)

            steps(sp, late, early)
            for parity in range(2):
                sp.wait_ge(sent[parity], 16 + 16 * TILES * TOPK * BATCHES // 2)

            def load_rows(e, j):
                sp.dma_start(xe[:, j], rows[bass.ds(e * CAPACITY, CAPACITY), :].rearrange("(t p) r -> p t r", p=128)
                             ).then_inc(xe_in[j], 16)

            for e in range(2):
                load_rows(e, e)

            def refill(e, j):
                sp.wait_ge(w1p_ok, e + 1)
                load_w1(e + 2, j)
                sp.wait_ge(xeT_ps, e + 1)
                sp.wait_ge(token_ok, e + 1)
                load_rows(e + 2, j)
                sp.wait_ge(ye_ps, e + 1)
                sp.wait_ge(yb_ok, e + 1)
                load_expert(e + 2, j)

            with sp.Fori(0, (EXPERTS - 2) // 2) as i:
                for j in range(2):
                    refill(2 * i + j, j)
            sp.wait_ge(added, 16 * SLOT_TILES * EXPERTS)

        @block.tensor
        def _(pe):
            mm, tr = nc.tensor.matmul, nc.tensor.transpose
            for free in free_from_start["pe"]:
                pe.sem_inc(free, 1)
            pe.wait_ge(wts_in, 16)
            pe.wait_ge(bv_ok, 1)
            mm(psC[:, 0:D], bv_rep[:], W[:, W_O:W_O + D], start=True, stop=True).then_inc(bias_ps, 1)
            pe.wait_ge(cst_in, 16)

            def heads(s, k, run):
                p = k % 2

                def x_transpose():
                    pe.wait_ge(xn1_ok, s + 3)
                    atleast(pe, mT_ok, 2 * s + 1, k + 1)
                    for t in range(TILES):
                        i = tr(psB[:, 128 * t:128 * t + 128], xn1[:, p, t], ident)
                    i.then_inc(xT_ps, 1)

                def project(cols, done):
                    pe.wait_ge(xT_ok, s + 3)
                    for n, c in enumerate(cols):
                        i = mm(psB[:, T * n:T * n + T], W[:, c:c + 128], xT[:, p], start=True, stop=True)
                    i.then_inc(done, 1)

                def project_v():
                    if live(k, 2):
                        pe.wait_ge(qs_ev, s + 3)
                    for t in range(TILES):
                        i = mm(psB[:, 128 * t:128 * t + 128], xT[:, 1 - p, 128 * t:128 * t + 128],
                               W[:, W_V:W_V + 128], start=True, stop=True)
                    i.then_inc(v_ps, 1)

                def max_transpose(half, b, kb, ps):
                    pe.wait_ge(mparts_ok, 2 * b + half + 1)
                    for t in range(TILES):
                        i = tr(ps[0:2 * HALF, 128 * t:128 * t + 128],
                               mparts[:, half, t].rearrange("p a h -> p (a h)").bitcast(fp32), ident)
                    i.then_inc(mT_ps, 1)

                def max_scores(h):
                    g = (s + 1) * HEADS + h
                    if h % HALF == 0:
                        pe.wait_ge(moved[h // HALF], 48 * (s + 2))
                    back = 1 if p == 1 and h < 2 else 2
                    atleast(pe, max_ok, g - back, (k + 1) * HEADS + h - back)
                    for t in range(TILES):
                        i = mm(max_bank(p, h)[:, T * t:T * t + T],
                               QK[1 - p][0:PART_ROWS, h, 0, 128 * t:128 * t + 128],
                               QK[1 - p][0:PART_ROWS, h, 1, :], start=True, stop=True)
                    i.then_inc(max_ps_ok, 1)

                def scores(h):
                    g = s * HEADS + h
                    if h % HALF == 0:
                        pe.wait_ge(max_in[h // HALF], 16 * (s + 1))
                    atleast(pe, prob_ok, g - 1, k * HEADS + h - 1)
                    for t in range(TILES):
                        i = mm(score_ps[h % 2][:, T * t:T * t + T], QK[p][0:SCORE_ROWS, h, 1, 128 * t:128 * t + 128],
                               QK[p][0:SCORE_ROWS, h, 0, :], start=True, stop=True)
                    i.then_inc(score_ok, 1)

                def values(b, kb, n):
                    grp, pos = n // 2, n % 2
                    pe.wait_ge(prob_ok, b * HEADS + 4 * n + 4)
                    if n == 0:
                        pe.wait_ge(v_ok, b + 1)
                        pe.wait_ge(mT_ok, 2 * b + 2)
                    for t in range(TILES):
                        c = V_BASE[2 * t + pos] + 128 * grp
                        for j in range(4):
                            i = mm(pv_ps[32 * j:32 * j + 32, T * grp:T * grp + T],
                                   VA[:, kb % 2, c + 32 * j:c + 32 * j + 32],
                                   P[:, (4 * n + j) % 8, T * t:T * t + T],
                                   start=(pos == 0 and t == 0), stop=(pos == 1 and t == 1))
                    i.then_inc(pv_ok, 1)

                out_ps = out_bank(k)

                def o_transpose():
                    pe.wait_ge(O_ok, s)
                    if k < BATCHES:
                        pe.wait_ge(hit_ok, s)
                    for t in range(TILES):
                        for g in range(2):
                            i = tr(out_ps[:, 256 * t + 128 * g:256 * t + 128 * g + 128],
                                   O[:, g, 128 * t:128 * t + 128], ident)
                    i.then_inc(Otr_ok, 1)

                def on_transpose():
                    pe.wait_ge(On_ok, s)
                    for t in range(TILES):
                        i = tr(out_ps[:, 128 * t:128 * t + 128], On[:, t], ident)
                    i.then_inc(OT_ps, 1)

                def project_out():
                    pe.wait_ge(OT_ok, s)
                    pe.wait_ge(xbias_ok, s + 1)
                    for t in range(TILES):
                        y = out_ps[:, 128 * t:128 * t + 128]
                        mm(y, OT[:, 128 * t:128 * t + 128], W[:, W_O:W_O + D], start=True, stop=False)
                        i = mm(y, ident, xbias[:, t], start=False, stop=True)
                    i.then_inc(y_ok, 1)

                def xn2_transpose():
                    pe.wait_ge(xn2_ok, s)
                    for t in range(TILES):
                        i = tr(psC[:, 128 * t:128 * t + 128], pay[:, p, 0, t, 0:D], ident)
                    i.then_inc(xn2T_ps, 1)

                def router():
                    pe.wait_ge(xn2T_ok, s - 1)
                    for t in range(TILES):
                        i = mm(logits(t), xn2T[:, 128 * t:128 * t + 128], W[:, W_R:W_R + EXPERTS],
                               start=True, stop=True)
                    i.then_inc(logit_ok, 1)

                def positions():
                    pe.wait_ge(chosen_ok, s - 1)
                    for t in range(TILES):
                        pos = psC[:, POS + EXPERTS * t:POS + EXPERTS * t + EXPERTS]
                        mm(pos, every[:], seen[:], start=True, stop=False)
                        for c in range(TOPK):
                            for u in range(t):
                                mm(pos, every[:], onehot[:, u, c], start=False, stop=False)
                            i = mm(pos, before[:], onehot[:, t, c], start=False, stop=(c == TOPK - 1))
                    i.then_inc(pos_ok, 1)

                for h in run:
                    if live(k, 0):
                        scores(h)
                    if live(k, 1):
                        max_scores(h)
                    if k == 0 and h == 0:
                        pe.wait_ge(ones_in, 32)
                        pe.wait_ge(attn_bias_ok, 1)
                        pe.wait_ge(before_ok, 1)
                    if h == 1 and live(k, 2):
                        x_transpose()
                    if h == 0 and live(k, -1):
                        values(s - 1, k - 1, 3)
                    if h == 4 and live(k, 0):
                        atleast(pe, O_ok, s, k)
                        max_transpose(1, s, k, pv_ps)
                    if h == at(k, 0, 1) and live(k, -2):
                        xn2_transpose()
                    if h == at(k, 2, 4) and live(k, -2):
                        router()
                    if h == 2 and live(k, 2):
                        project((W_Q, W_K), qk_ps)
                    if h == 4 and live(k, 2):
                        pe.wait_ge(qk_ev, s + 3)
                        project((W_QS, W_KS), qs_ps)
                    if h == 5 and live(k, -2):
                        positions()
                    if h == 5 and live(k, 0):
                        values(s, k, 0)
                    if h == at(k, 6, 1) and live(k, -1):
                        o_transpose()
                    if h == 7 and live(k, 1):
                        project_v()
                    if h == at(k, 10, 2) and live(k, -1):
                        on_transpose()
                    if h == 9 and live(k, 0):
                        values(s, k, 1)
                    if h == at(k, 11, 4) and live(k, -1):
                        project_out()
                    if h == 10 and live(k, 1):
                        pe.wait_ge(v_ok, s + 2)
                        max_transpose(0, s + 1, k + 1, psB)
                    if h == 13 and live(k, 0):
                        values(s, k, 2)

            steps(pe, *by_heads(heads))

            pe.wait_ge(prob_ok, BATCHES * HEADS)
            pe.wait_ge(max_ok, BATCHES * HEADS)
            pe.wait_ge(mT_ok, 2 * BATCHES)
            pe.wait_ge(O_ok, BATCHES)

            def gather(e, j, turn):
                pe.wait_ge(xe_in[j], 16 * (turn + 1))
                if not is_number(e, 0):
                    pe.wait_ge(xelo_ok, e)
                for t in range(SLOT_TILES):
                    last = tr(bank[4][:, 128 * t:128 * t + 128], xe[:, j, t, 0:D], ident)
                last.then_inc(xeT_ps, 1)

            def expert(e, j, turn):
                if is_number(e, 0):
                    gather(0, 0, 0)
                pe.wait_ge(xeT_ok, e + 1)
                pe.wait_ge(w1p_ok, e + 1)
                for c in range(CHUNKS):
                    h, cols = bank[c][:, 0:CAPACITY], slice(128 * c, 128 * c + 128)
                    mm(h, w1p[:, j, 0, cols], xeT[:, j, 0], start=True, stop=False)
                    mm(h, w1p[:, j, 1, cols], xeT[:, j, 0], start=False, stop=False)
                    if c == 0:
                        pe.wait_ge(xelo_ok, e + 1)
                    mm(h, w1p[:, j, 0, cols], xeT[:, j, 1], start=False, stop=True).then_inc(h_ps, 1)
                if not is_number(e, EXPERTS - 1):
                    gather(e + 1, 1 - j, turn + j)
                pe.wait_ge(w_in[j], 48 * (turn + 1))
                if not is_number(e, 0):
                    pe.wait_ge(yb_ok, e)
                for t in range(SLOT_TILES):
                    for c in range(CHUNKS):
                        if t == 0:
                            pe.wait_ge(hV_ok if c % 2 else hA_ok, 2 * e + c // 2 + 1)
                        ye = bank[5 + t] if is_number(e, EXPERTS - 1) else bank[5]
                        last = mm(ye[:, 128 * t:128 * t + 128], hT[:, c, 128 * t:128 * t + 128],
                                  w2s[:, j, c], start=(c == 0), stop=(c == CHUNKS - 1))
                    if t == SLOT_TILES - 1 or is_number(e, EXPERTS - 1):
                        last.then_inc(ye_ps, 1)

            experts(pe, expert)

        @block.scalar
        def _(act):
            fn = nc.scalar.activation
            for free in free_from_start["act"]:
                act.sem_inc(free, 1)
            act.wait_ge(ones_set, 1)
            fn(warm[0:2 * HEADS], ones[:, 0:1], ACT.Exp)
            act.wait_ge(va_set, 1)

            def heads(s, k, run):
                p = k % 2

                def probs(h):
                    g = s * HEADS + h
                    act.wait_ge(score_ok, g + 1)
                    if h % 4 == 0:
                        atleast(act, pv_ok, 4 * s + h // 4 - 1, 4 * k + h // 4 - 1)
                    fn(P[:, h % 8], score_ps[h % 2][:], ACT.Exp, scale=float(HD) ** -0.5).then_inc(prob_ok, 1)

                def copy_max(half, b, ps):
                    act.wait_ge(mT_ps, 2 * b + half + 1)
                    atleast(act, max_in[half], 16 * b, k + 1 - half)
                    fn(mT[:, half], ps[0:2 * HALF, 0:T], ACT.Copy).then_inc(mT_ok, 1)

                def copy_x():
                    act.wait_ge(xT_ps, s + 3)
                    atleast(act, v_ps, s + 1, k + 1)
                    fn(xT[:, p], psB[:, 0:T], ACT.Copy).then_inc(xT_ok, 1)

                def copy_v():
                    act.wait_ge(v_ps, s + 2)
                    atleast(act, pv_ok, 4 * s, k)
                    v = VA[:, 1 - p].rearrange("p (i r) -> p i r", r=V_STEP)[:, :, 0:256]
                    fn(v.rearrange("p i (g c) -> p i g c", c=32)[:, :, :, 0:HD],
                       psB[:, 0:2 * 128].rearrange("p (i g c) -> p i g c", i=4, c=HD), ACT.Copy).then_inc(v_ok, 1)

                def norm1():
                    b = (k + 3) % 2
                    act.wait_ge(shift1_ok, s + 4)
                    atleast(act, xT_ps, s + 2, k + 2)
                    for t in range(TILES):
                        i = fn(xn1[:, b, t], xin[:, b, t], ACT.Identity, bias=shift1[:, b, t:t + 1],
                               scale=rstd1[:, b, t:t + 1])
                    i.then_inc(xn1_ok, 1)

                def norm2():
                    act.wait_ge(shift2_ok, s)
                    for t in range(TILES):
                        i = fn(pay[:, 1 - p, 0, t, 0:D], x1[:, t], ACT.Identity, bias=shift2[:, t:t + 1],
                               scale=rstd2[:, t:t + 1])
                    i.then_inc(xn2_ok, 1)

                def copy_o():
                    act.wait_ge(pv_ok, 4 * s)
                    act.wait_ge(Otr_ok, s)
                    fn(O[:].rearrange("p g t -> p (g t)"), pv_ps[:], ACT.Copy).then_inc(O_ok, 1)

                def copy_on():
                    act.wait_ge(OT_ps, s + 1)
                    fn(OT[:], out_bank(k)[:, 0:T], ACT.Copy).then_inc(OT_ok, 1)

                def copy_xn2():
                    act.wait_ge(xn2T_ps, s - 1)
                    fn(xn2T[:], psC[:, 0:T], ACT.Copy).then_inc(xn2T_ok, 1)

                def copy_x1():
                    act.wait_ge(y_ok, s)
                    act.wait_ge(xn2_ok, s)
                    act.wait_ge(tail_dma, 16 * (2 * s - 1))
                    fn(x1[:].rearrange("p t d -> p (t d)"), out_bank(k)[:, 0:T], ACT.Copy).then_inc(x1_ok, 1)

                def second_rows():
                    act.wait_ge(xn2_ok, s)
                    fn(pay[:, p, 1, :, 0:D], pay[:, p, 0, :, 0:D], ACT.Copy).then_inc(rows2_ok, 1)

                def exp_gap():
                    act.wait_ge(gap_ok, s - 1)
                    fn(e2[:], gap[:], ACT.Exp).then_inc(e2_ok, 1)

                for h in run:
                    if live(k, 0):
                        probs(h)
                    if h == at(k, 2, 1) and live(k, -1):
                        copy_o()
                    if h == 1 and live(k, 2):
                        copy_x()
                    if h == 3 and live(k, 0):
                        copy_max(1, s, pv_ps)
                    if h == at(k, 0, 2) and live(k, -2):
                        copy_xn2()
                    if h == at(k, 4, 2) and live(k, -2):
                        second_rows()
                    if h == at(k, 3, 4) and live(k, -2):
                        exp_gap()
                    if h == at(k, 10, 2) and live(k, -1):
                        copy_on()
                    if h == 9 and live(k, 1):
                        copy_v()
                    if h == 14 and live(k, 3):
                        norm1()
                    if h == 11 and live(k, 1):
                        copy_max(0, s + 1, psB)
                    if h == at(k, 11, 2) and live(k, -1):
                        copy_x1()
                    if h == at(k, 15, 5) and live(k, -1):
                        norm2()

            steps(act, *by_heads(heads))

            def expert(e, j, turn):
                act.wait_ge(xeT_ps, e + 1)
                fn(xeT[:, j, 0], bank[4][:, 0:CAPACITY], ACT.Copy).then_inc(xeT_ok, 1)
                act.wait_ge(w_in[j], 48 * (turn + 1))
                for c in (0, 2):
                    act.wait_ge(h_ps, 4 * e + c + 1)
                    if not is_number(e, 0):
                        act.wait_ge(ye_ps, e)
                    fn(hT[:, c], bank[c][:, 0:CAPACITY], ACT.Relu, bias=b1s[:, j, c:c + 1]).then_inc(hA_ok, 1)

            experts(act, expert)

        @block.vector
        def _(dve):
            V = nc.vector
            count = Count(DVE_LINKS)

            def link(ins, alone=False):
                ins.then_inc(dve_chain, 1)
                dve.wait_ge(dve_chain, count.next())
                if alone:
                    apart(dve, dve_passed)

            for free in free_from_start["dve"]:
                dve.sem_inc(free, 1)
            V.memset(ones[:], 1.0).then_inc(ones_set, 1)
            link(V.memset(VA[:], 0.0))
            for p in range(2):
                for n in range(4):
                    c = V_BASE[n] + 9 * (n % 2) + HD
                    i = V.memset(VA[:, p, c:c + 32 * 7 + 1:32], 1.0)
            i.then_inc(va_set, 1)
            V.memset(seen[:], 0.0)

            def first_constants():
                dve.wait_ge(wts_in, 16)
                V.tensor_copy(bv_rep[:], W[:, W_BV:W_BV + 1].to_broadcast([128, 128])).then_inc(bv_ok, 1)
                V.memset(every[:], 1.0)
                V.tensor_copy(before[:], C[:, C_UP:C_UP + 128]).then_inc(before_ok, 1)

            def second_constants():
                dve.wait_ge(bias_ps, 1)
                dve.wait_ge(bo_in, 16)
                V.tensor_tensor(attn_bias[:], psC[:, 0:D], bo_all[:], ALU.add).then_inc(attn_bias_ok, 1)

            def heads(s, k, run):
                p = k % 2

                def reduce(h):
                    g = (s + 1) * HEADS + h
                    dve.wait_ge(max_ps_ok, g + 1)
                    if h % HALF == 0:
                        atleast(dve, mparts_ok, 2 * (s + 1) + h // HALF - 1, k + 1)
                    V.tensor_reduce(negmax[:, h // HALF, :, h % HALF],
                                    max_bank(p, h)[:].rearrange("p (t k) -> p t k", t=TILES),
                                    axis=AX.X, op=ALU.max, negate=True).then_inc(max_ok, 1)

                def norm1_stats():
                    b = (k + 3) % 2
                    dve.wait_ge(x_in[b], 16 * pair(s, k, 3))
                    atleast(dve, xn1_ok, s + 2, k + 2)
                    for t in range(TILES):
                        i = V.bn_stats(stats1[:, b, t], xin[:, b, t])
                    link(i, True)
                    for t in range(TILES):
                        i = V.bn_aggr(mv1[:, b, t], stats1[:, b, t])
                    i.then_inc(stats1_ok, 1)

                def shift_norm1():
                    b = (k + 3) % 2
                    dve.wait_ge(rstd1_ok, s + 4)
                    V.scalar_tensor_tensor(out=shift1[:, b], in0=mv1[:, b, :, 0], scalar=-1.0, in1=rstd1[:, b],
                                           op0=ALU.mult, op1=ALU.mult).then_inc(shift1_ok, 1)

                def shift_norm2():
                    dve.wait_ge(rstd2_ok, s)
                    dve.wait_ge(xn2_ok, s)
                    V.scalar_tensor_tensor(out=shift2[:], in0=mv2[:, :, 0], scalar=-1.0, in1=rstd2[:],
                                           op0=ALU.mult, op1=ALU.mult).then_inc(shift2_ok, 1)

                def rotate(ready, first, table, into, done):
                    dve.wait_ge(ready, s + 3)
                    atleast(dve, rope_ok, s + 2, k + 2)
                    for n in range(2):
                        i = V.scalar_tensor_tensor(
                            out=into[:, n], in0=psB[:, T * n:T * n + T],
                            scalar=W[:, W_BIAS + first + n:W_BIAS + first + n + 1], in1=C[:, table:table + T],
                            op0=ALU.add, op1=ALU.mult)
                    i.then_inc(done, 1)

                def normalise():
                    dve.wait_ge(Otr_ok, s + 1)
                    o = out_bank(k)[:].rearrange("p (a c) -> p a c", c=32)[:, :, 0:18].rearrange(
                        "p a (b r) -> p a b r", r=HD + 1)
                    link(V.reciprocal(rsum[:].unsqueeze(3), o[:, :, :, HD:HD + 1]))
                    dve.wait_ge(OT_ps, s)
                    V.tensor_tensor(On[:].rearrange("p t (a b d) -> p (t a) b d", b=2, d=HD), o[:, :, :, 0:HD],
                                    rsum[:].unsqueeze(3).to_broadcast([128, TILES * 8, 2, HD]), ALU.mult
                                    ).then_inc(On_ok, 1)

                def norm2_stats():
                    dve.wait_ge(x1_ok, s + 1)
                    dve.wait_ge(pay_ok, s)
                    for t in range(TILES):
                        i = V.bn_stats(stats2[:, t], x1[:, t])
                    link(i, True)
                    for t in range(TILES):
                        i = V.bn_aggr(mv2[:, t], stats2[:, t])
                    i.then_inc(stats2_ok, 1)

                def choose():
                    dve.wait_ge(logit_ok, s - 1)
                    apart(dve, dve_passed)
                    for t in range(TILES):
                        i = V.max(best[:, t], logits(t))
                    link(i, True)
                    for t in range(TILES):
                        i = V.max_index(besti[:, t], best[:, t], logits(t))
                    V.tensor_tensor(gap[:], best[:, :, 1], best[:, :, 0], ALU.subtract).then_inc(gap_ok, 1)
                    dve.wait_ge(gap_ok, s - 1)
                    V.tensor_tensor(
                        onehot[:], besti[:, :, 0:TOPK].unsqueeze(3).to_broadcast([128, TILES, TOPK, EXPERTS]),
                        C[:, C_IOTA:C_IOTA + TILES * TOPK * EXPERTS].rearrange("p (t k e) -> p t k e", t=TILES, k=TOPK),
                        ALU.is_equal).then_inc(chosen_ok, 1)

                def place():
                    dve.wait_ge(pos_ok, s - 1)
                    dve.wait_ge(e2_ok, s - 1)
                    dve.wait_ge(pay_ok, s)
                    for t in range(TILES):
                        i = V.tensor_tensor(
                            hit[:, t], onehot[:, t],
                            psC[:, POS + EXPERTS * t:POS + EXPERTS * t + EXPERTS].unsqueeze(1).to_broadcast(
                                [128, TOPK, EXPERTS]), ALU.mult)
                    i.then_inc(hit_ok, 1)
                    dve.wait_ge(hit_ok, s)
                    V.tensor_reduce(slot[:], hit[:], axis=AX.X, op=ALU.add)
                    V.tensor_reduce(chosen[:], onehot[:].rearrange("p t k e -> p e (t k)"), axis=AX.X, op=ALU.add)
                    link(V.tensor_scalar(den[:], e2[:], 1.0, None, ALU.add))
                    V.tensor_scalar(over[:], slot[:], float(CAPACITY), float(NOWHERE), ALU.is_ge, ALU.mult)
                    V.scalar_tensor_tensor(out=base[:], in0=besti[:, :, 0:TOPK], scalar=float(CAPACITY), in1=slot[:],
                                           op0=ALU.mult, op1=ALU.add)
                    link(V.reciprocal(pay[:, p, 0, :, D:D + 1], den[:].unsqueeze(2)))
                    V.tensor_tensor(dest[:, p], base[:], over[:], ALU.add)
                    V.tensor_tensor(seen[:], seen[:], chosen[:], ALU.add)
                    V.tensor_tensor(pay[:, p, 1, :, D], pay[:, p, 0, :, D], e2[:], ALU.mult).then_inc(slot_ok, 1)

                for h in run:
                    if live(k, 1):
                        reduce(h)
                    if h == 2 and live(k, -2):
                        choose()
                    if h == 2 and live(k, 2):
                        rotate(qk_ps, 0, C_COS, rot1, qk_ev)
                    if h == 4 and live(k, 2):
                        rotate(qs_ps, 2, C_SIN, rot2, qs_ev)
                        if k == -2:
                            split_rope(dve, V, dve_passed, s, k)
                    if h == 5 and live(k, -2):
                        place()
                    if h == at(k, 7, 0) and live(k, -1):
                        normalise()
                    if h == 8 and live(k, 3):
                        norm1_stats()
                    if h == 12 and live(k, 3):
                        shift_norm1()
                    if h == at(k, 11, 3) and live(k, -1):
                        norm2_stats()
                    if h == at(k, 14, 5) and live(k, -1):
                        shift_norm2()
                    if h == HEADS - 1 and k == -3:
                        first_constants()
                    if h == HEADS - 1 and k == -2:
                        second_constants()
                        V.memset(QK[1][0:PART_ROWS, HALF:HEADS].bitcast(fp32), 0.0).then_inc(zero_ok[1][1], 1)

            steps(dve, *by_heads(heads), count)

            def split_w1(e, j, turn):
                dve.wait_ge(w1_in[j], 16 * (turn + 1))
                V.tensor_copy(w1p[:, j, 0], w1s[:, j]).then_inc(w1hi_ok, 1)
                dve.wait_ge(w1hi_ok, e + 1)
                V.tensor_tensor(w1p[:, j, 1], w1s[:, j], w1p[:, j, 0].bitcast(fp32), ALU.subtract).then_inc(w1p_ok, 1)

            def split_x(e, j):
                dve.wait_ge(xeT_ok, e + 1)
                V.tensor_tensor(xeT[:, j, 1], bank[4][:, 0:CAPACITY], xeT[:, j, 0].bitcast(fp32), ALU.subtract
                                ).then_inc(xelo_ok, 1)

            def expert(e, j, turn):
                if is_number(e, 0):
                    split_w1(0, 0, 0)
                    split_x(0, 0)
                dve.wait_ge(w_in[j], 48 * (turn + 1))
                for c in (1, 3):
                    dve.wait_ge(h_ps, 4 * e + c + 1)
                    if not is_number(e, 0):
                        dve.wait_ge(ye_ps, e)
                    V.tensor_scalar(hT[:, c], bank[c][:, 0:CAPACITY], b1s[:, j, c:c + 1], 0.0, ALU.add, ALU.max
                                    ).then_inc(hV_ok, 1)
                if is_number(e, EXPERTS - 1):
                    for t in range(SLOT_TILES):
                        dve.wait_ge(ye_ps, e + 1 + t)
                        V.tensor_tensor(yb[:, t], bank[5 + t][:, D * t:D * t + D], b2s[:, j], ALU.add).then_inc(yb_ok, 1)
                        dve.wait_ge(yb_ok, e + 1 + t)
                        dve.wait_ge(token_ok, e + 1)
                        dve.wait_ge(added, 16 * SLOT_TILES * (e - 1))
                        V.tensor_tensor(yg[:, j, t], yb[:, t], gate[:, j, t:t + 1].to_broadcast([128, D]), ALU.mult
                                        ).then_inc(yg_ok, 1)
                    return
                split_w1(e + 1, 1 - j, turn + j)
                split_x(e + 1, 1 - j)
                dve.wait_ge(ye_ps, e + 1)
                V.tensor_tensor(yb[:], bank[5][:, 0:CAPACITY].rearrange("p (t d) -> p t d", d=D),
                                b2s[:, j].unsqueeze(1).to_broadcast([128, SLOT_TILES, D]), ALU.add
                                ).then_inc(yb_ok, 1)
                dve.wait_ge(yb_ok, e + 1)
                dve.wait_ge(token_ok, e + 1)
                V.tensor_tensor(yg[:, j], yb[:], gate[:, j].unsqueeze(2).to_broadcast([128, SLOT_TILES, D]), ALU.mult
                                ).then_inc(yg_ok, 1)

            experts(dve, expert)

        @block.gpsimd
        def _(pool):
            G = nc.gpsimd
            count = Count(POOL_LINKS)

            def link(ins):
                ins.then_inc(pool_chain, 1)
                pool.wait_ge(pool_chain, count.next())
                apart(pool, pool_passed)

            for free in free_from_start["pool"]:
                pool.sem_inc(free, 1)
            G.memset(QK[0][0:PART_ROWS, 0:HALF].bitcast(fp32), 0.0).then_inc(zero_ok[0][0], 1)
            link(G.memset(minus_half[:], -0.5))

            def inverse_deviation(mv, rstd, done):
                link(G.tensor_scalar(rstd, mv[:, :, 1], 1.0, EPS, ALU.mult, ALU.add))
                G.tensor_tensor(rstd, rstd, minus_half[:], ALU.pow).then_inc(done, 1)

            def deviation1(s, k):
                b = (k + 3) % 2
                pool.wait_ge(stats1_ok, s + 4)
                apart(pool, pool_passed)
                inverse_deviation(mv1[:, b], rstd1[:, b], rstd1_ok)

            def add_residual(s, k):
                pool.wait_ge(tail_dma, 16 * (2 * s - 1))
                atleast(pool, y_ok, s - 1, k - 1)
                if k == 1:
                    pool.wait_ge(attn_bias_ok, 1)
                G.tensor_tensor(xbias[:], xres[:], attn_bias[:].unsqueeze(1).to_broadcast([128, TILES, D]), ALU.add
                                ).then_inc(xbias_ok, 1)

            def deviation2(s, k):
                p = (k - 1) % 2
                pool.wait_ge(stats2_ok, s)
                pool.wait_ge(sent[p], 16 + 16 * TILES * TOPK * pair(s, k, -3))
                if k == 1:
                    pool.wait_ge(sent[1 - p], 16)
                apart(pool, pool_passed)
                inverse_deviation(mv2[:], rstd2[:], rstd2_ok)
                link(G.tensor_copy(pay[:, p, :, :, D + 1].bitcast(i32), tok[:].unsqueeze(1).to_broadcast(
                    [128, TOPK, TILES])))
                G.tensor_scalar(tok[:], tok[:], 1.0, float(T), ALU.mult, ALU.add).then_inc(pay_ok, 1)

            def dispatch(s, k):
                p = k % 2
                pool.wait_ge(slot_ok, s - 1)
                pool.wait_ge(rows2_ok, s - 1)
                apart(pool, pool_passed)
                for c in range(TOPK):
                    for t in range(TILES):
                        G.indirect_dma_start(
                            out=rows, out_offset=bass.IndirectOffsetOnAxis(ap=dest[:, p, t, c:c + 1], axis=0),
                            in_=pay[:, p, c, t], in_offset=None, bounds_check=SLOTS - 1, oob_is_err=False,
                        ).then_inc(sent[p], 16)

            def split_max(s, k, half):
                pool.wait_ge(max_ok, (s + 1) * HEADS + (half + 1) * HALF)
                atleast(pool, mT_ps, 2 * (s + 1) + half - 1, k + 1)
                apart(pool, pool_passed)
                link(G.tensor_scalar(mparts[:, half, :, 0], negmax[:, half], 1.0, 0.0, ALU.mult, ALU.add))
                G.tensor_tensor(mparts[:, half, :, 1], negmax[:, half], mparts[:, half, :, 0].bitcast(fp32),
                                ALU.subtract).then_inc(mparts_ok, 1)

            def early(s, k):
                if live(k, 0):
                    split_max(s - 1, k - 1, 1)
                if live(k, -1):
                    add_residual(s, k)
                if live(k, 2) and k > -2:
                    split_rope(pool, G, pool_passed, s, k)
                if live(k, 1):
                    split_max(s, k, 0)
                if live(k, -2) and k != BATCHES:
                    dispatch(s, k)

            def late(s, k):
                if live(k, 3):
                    deviation1(s, k)
                if live(k, -1):
                    deviation2(s, k)
                if k == BATCHES:
                    dispatch(s, k)
                if k == -2:
                    G.memset(QK[1][0:PART_ROWS, 0:HALF].bitcast(fp32), 0.0).then_inc(zero_ok[1][0], 1)
                if k == -3:
                    G.memset(QK[0][0:PART_ROWS, HALF:HEADS].bitcast(fp32), 0.0).then_inc(zero_ok[0][1], 1)
                    link(G.memset(blank[:], 0.0))
                    pool.wait_ge(cst_in, 16)
                    G.tensor_copy(blank[:, :, D + 1].bitcast(i32), C[:, C_SPARE:C_SPARE + SLOT_TILES]
                                  ).then_inc(blank_set, 1)
                    pool.wait_ge(blank_set, 1)
                    for n in range(2):
                        G.dma_start(
                            rows.rearrange("(n e p t) r -> n p e (t r)", n=2, t=SLOT_TILES, p=128)[n],
                            blank[:].rearrange("p t r -> p (t r)").unsqueeze(1).to_broadcast(
                                [128, EXPERTS // 2, SLOT_TILES * ROW])).then_inc(sent[n], 16)
                    G.dma_start(out[TOKENS:OUT_ROWS, :].rearrange("(t p) d -> p t d", p=128), blank[:, :, 0:D]
                                ).then_inc(spare_ok, 16)
                    link(G.tensor_copy(tok[:], C[:, C_TOK:C_TOK + TILES]))

            steps(pool, late, early, count)
            pool.wait_ge(tail_dma, 16 * 2 * BATCHES)
            pool.wait_ge(spare_ok, 16)

            def copy_tokens(e, j, turn):
                pool.wait_ge(xe_in[j], 16 * (turn + 1))
                apart(pool, pool_passed)
                G.tensor_copy(gate[:, j], xe[:, j, :, D])
                G.tensor_copy(token[:, j], xe[:, j, :, D + 1].bitcast(i32)).then_inc(token_ok, 1)

            def add_rows(j, t):
                G.indirect_dma_start(
                    out=out, out_offset=bass.IndirectOffsetOnAxis(ap=token[:, j, t:t + 1], axis=0),
                    in_=yg[:, j, t], in_offset=None, bounds_check=OUT_ROWS - 1, oob_is_err=True,
                    compute_op=ALU.add).then_inc(added, 16)

            def expert(e, j, turn):
                if is_number(e, 0):
                    copy_tokens(0, 0, 0)
                if is_number(e, EXPERTS - 1):
                    pool.wait_ge(added, 16 * SLOT_TILES * e)
                    for t in range(SLOT_TILES):
                        pool.wait_ge(yg_ok, e + 1 + t)
                        add_rows(j, t)
                    return
                if not is_number(e, 0):
                    pool.wait_ge(added, 16 * SLOT_TILES * e)
                copy_tokens(e + 1, 1 - j, turn + j)
                pool.wait_ge(yg_ok, e + 1)
                apart(pool, pool_passed)
                for t in range(SLOT_TILES):
                    add_rows(j, t)

            experts(pool, expert)


def kernel(**inputs):
    import numpy as np
    import concourse.bacc as bacc
    from concourse.bass_utils import run_bass_kernel_spmd

    f = {n: np.asarray(a) for n, a in inputs.items()}
    qk = np.arange(D).reshape(2, HALF, HD).transpose(0, 2, 1).ravel()
    swapped = np.arange(D).reshape(2, HALF, HD)[:, :, np.arange(HD) ^ 1].transpose(0, 2, 1).ravel()
    vcols = np.arange(D).reshape(2, 2, 4, HD).transpose(1, 0, 2, 3).ravel()
    orows = np.arange(D).reshape(2, 2, 4, HD).transpose(0, 2, 1, 3).ravel()
    p = "L0_attn_"
    wq, wk, wv, wo = (f[p + n] for n in ("Wq", "Wk", "Wv", "Wo"))
    bq, bk, bv = (f[p + n] for n in ("bq", "bk", "bv"))
    wts = np.concatenate([
        wq[qk].T, wk[qk].T, wq[swapped].T, wk[swapped].T, wv[vcols].T, wo[:, orows].T, f["L0_ffn_w_router"],
        bq[qk][:, None], bk[qk][:, None], bq[swapped][:, None], bk[swapped][:, None], bv[orows][:, None]], axis=1)

    freq = (np.float32(1) / np.float32(10000) ** (np.arange(0, HD, 2, dtype=np.float32) / np.float32(HD)))
    angle = np.repeat(np.arange(T, dtype=np.float32)[:, None] * freq[None, :], 2, axis=-1).astype(np.float32)
    cos, sin = np.cos(angle), np.sin(angle) * np.where(np.arange(HD) % 2 == 0, -1, 1).astype(np.float32)
    row_feature = np.tile(np.repeat(np.arange(HD), HALF), 2)
    part = np.arange(128)
    cst = np.concatenate([
        np.eye(128), cos.T[row_feature], sin.T[row_feature], part[:, None] < part[None, :],
        np.tile(np.arange(EXPERTS), (128, TILES * TOPK)), part[:, None] + 128 * np.arange(TILES)[None, :],
        TOKENS + SLOT_TILES * part[:, None] + np.arange(SLOT_TILES)[None, :],
    ], axis=1).astype(np.float32)

    arrays = {
        "x": f[p + "x"].reshape(TOKENS, D), "wts": wts, "cst": cst, "bo": f[p + "bo"],
        "w1": f["L0_ffn_w1"].reshape(EXPERTS * D, HIDDEN),
        "b1": f["L0_ffn_b1"].reshape(EXPERTS, CHUNKS, 128).transpose(0, 2, 1).reshape(EXPERTS * 128, CHUNKS),
        "w2": f["L0_ffn_w2"].reshape(EXPERTS * HIDDEN, D), "b2": f["L0_ffn_b2"],
    }
    arrays = {n: np.ascontiguousarray(a) for n, a in arrays.items()}
    nc = bacc.Bacc("TRN2", target_bir_lowering=False, num_devices=1)
    args = {n: nc.dram_tensor(n, a.shape, mybir.dt.from_np(a.dtype), kind="ExternalInput").ap()
            for n, a in arrays.items()}
    out = nc.dram_tensor("out", (OUT_ROWS, D), mybir.dt.float32, kind="ExternalOutput").ap()
    rows = nc.dram_tensor("rows", (SLOTS, ROW), mybir.dt.float32, kind="Internal").ap()
    build(nc, **args, out=out, rows=rows)
    r = run_bass_kernel_spmd(nc, [arrays], core_ids=[0])
    return r.results[0]["out"][:TOKENS].reshape(BATCHES, T, D)
```
